# Optimizing a Trainium2 kernel written in Bass

```python
import numpy as np
import jax
import jax.numpy as jnp

def _softmax(x, axis=-1):
    return jax.nn.softmax(x, axis=axis)

def _gelu(x):
    return jax.nn.gelu(x, approximate=True)

def _silu(x):
    return jax.nn.silu(x)

def _sigmoid(x):
    return jax.nn.sigmoid(x)

def _layernorm(x, axis=-1, eps=1e-05):
    m = jnp.mean(x, axis=axis, keepdims=True)
    v = jnp.var(x, axis=axis, keepdims=True)
    return (x - m) / jnp.sqrt(v + eps)

def _scatter_add(tgt, idx, src, axis=0):
    return tgt.at[idx].add(src)

def _segment_sum(src, seg, n):
    return jax.ops.segment_sum(src, seg, n)
kernel_name = 'mk_xattn_seq_d2_seqx_r2_c9be3d'

def setup_inputs(seed: int=0):
    np.random.seed(seed)
    _w = jnp.asarray

    def _rec_inputs():
        import jax
        import jax.numpy as jnp
        _rk = jax.random.key(seed)
        x = -0.0002928 + 1 * jax.random.normal(jax.random.fold_in(_rk, 1), (8, 100, 512), jnp.float32)
        _lenS = 100 - jax.random.randint(jax.random.fold_in(_rk, 7), (8,), 0, max(1, 100 // 4) + 1, jnp.int32)
        _lenS2 = 722 - jax.random.randint(jax.random.fold_in(_rk, 8), (8,), 0, max(1, 722 // 4) + 1, jnp.int32)
        _ctx_1024P = jax.random.normal(jax.random.fold_in(_rk, 11), (8, 16, 512), jnp.float32)
        _ctx_1024c = jax.random.dirichlet(jax.random.fold_in(_rk, 511), 0.3 * jnp.ones((16,), jnp.float32), (8, 722))
        _ctx_1024t = jnp.einsum('bsk,bkd->bsd', _ctx_1024c, _ctx_1024P)
        _ctx_1024t = _ctx_1024t * jax.lax.rsqrt(jnp.mean(jnp.square(_ctx_1024t)) + 1e-12) * 0.953939
        ctx_1024 = 4.13588e-05 + 0.999923 * (_ctx_1024t + 0.3 * jax.random.normal(jax.random.fold_in(_rk, 611), (8, 722, 512), jnp.float32))
        return (x, ctx_1024)
    x, ctx_1024 = _rec_inputs()

    def _L0_xattn_setup():
        import jax, jax.numpy as jnp
        import numpy as np
        E = 512
        H = 16
        HD = E // H
        EPS = 1e-05

        def _layer_norm(x, g, b):
            mu = jnp.mean(x, axis=-1, keepdims=True)
            var = jnp.var(x, axis=-1, keepdims=True)
            return (x - mu) * jax.lax.rsqrt(var + EPS) * g + b
        key = jax.random.key(seed)
        ks = jax.random.split(key, 16)
        s = 0.02
        inp = {'query': jax.random.normal(ks[0], (4, 512, E), jnp.float32), 'key': jax.random.normal(ks[1], (4, 1024, E), jnp.float32), 'value': jax.random.normal(ks[2], (4, 1024, E), jnp.float32), 'wq': jax.random.normal(ks[3], (E, E), jnp.float32) * s, 'bq': jnp.zeros((E,), jnp.float32), 'wk': jax.random.normal(ks[4], (E, E), jnp.float32) * s, 'bk': jnp.zeros((E,), jnp.float32), 'wv': jax.random.normal(ks[5], (E, E), jnp.float32) * s, 'bv': jnp.zeros((E,), jnp.float32), 'wo': jax.random.normal(ks[6], (E, E), jnp.float32) * s, 'bo': jnp.zeros((E,), jnp.float32), 'ln1_g': jnp.ones((E,), jnp.float32), 'ln1_b': jnp.zeros((E,), jnp.float32), 'ln2_g': jnp.ones((E,), jnp.float32), 'ln2_b': jnp.zeros((E,), jnp.float32), 'w1': jax.random.normal(ks[7], (E, 4 * E), jnp.float32) * s, 'b1': jnp.zeros((4 * E,), jnp.float32), 'w2': jax.random.normal(ks[8], (4 * E, E), jnp.float32) * s, 'b2': jnp.zeros((E,), jnp.float32)}
        return inp
    _L0_xattn_all = _L0_xattn_setup()
    _L0_xattn_in = {k: v for k, v in _L0_xattn_all.items() if k in ('wq', 'bq', 'wk', 'bk', 'wv', 'bv', 'wo', 'bo', 'ln1_g', 'ln1_b', 'ln2_g', 'ln2_b', 'w1', 'b1', 'w2', 'b2')}
    del _L0_xattn_all

    def _L1_xattn_setup():
        import jax, jax.numpy as jnp
        import numpy as np
        B, S, D = (4, 1024, 512)
        H, DK, DV = (16, 64, 64)
        GRAPH_ATTN_BIAS = 2.0
        POS_WIN = 4.0
        LN_EPS = 1e-06
        key = jax.random.key(seed)
        ks = jax.random.split(key, 9)
        init = 0.02
        return {'q': jax.random.normal(ks[0], (B, S, D), jnp.float32), 'k': jax.random.normal(ks[1], (B, S, D), jnp.float32), 'v': jax.random.normal(ks[2], (B, S, D), jnp.float32), 'Wq': jax.random.normal(ks[3], (D, H * DK), jnp.float32) * init, 'Wk': jax.random.normal(ks[4], (D, H * DK), jnp.float32) * init, 'Wv': jax.random.normal(ks[5], (D, H * DV), jnp.float32) * init, 'Wfc': jax.random.normal(ks[6], (H * DV, D), jnp.float32) * init, 'gamma': jnp.ones((D,), jnp.float32), 'beta': jnp.zeros((D,), jnp.float32)}
    _L1_xattn_all = _L1_xattn_setup()
    _L1_xattn_in = {k: v for k, v in _L1_xattn_all.items() if k in ('Wq', 'Wk', 'Wv', 'Wfc', 'gamma', 'beta')}
    del _L1_xattn_all
    return {'x': x, 'ctx_1024': ctx_1024, 'L0_xattn_wq': _L0_xattn_in['wq'], 'L0_xattn_bq': _L0_xattn_in['bq'], 'L0_xattn_wk': _L0_xattn_in['wk'], 'L0_xattn_bk': _L0_xattn_in['bk'], 'L0_xattn_wv': _L0_xattn_in['wv'], 'L0_xattn_bv': _L0_xattn_in['bv'], 'L0_xattn_wo': _L0_xattn_in['wo'], 'L0_xattn_bo': _L0_xattn_in['bo'], 'L0_xattn_ln1_g': _L0_xattn_in['ln1_g'], 'L0_xattn_ln1_b': _L0_xattn_in['ln1_b'], 'L0_xattn_ln2_g': _L0_xattn_in['ln2_g'], 'L0_xattn_ln2_b': _L0_xattn_in['ln2_b'], 'L0_xattn_w1': _L0_xattn_in['w1'], 'L0_xattn_b1': _L0_xattn_in['b1'], 'L0_xattn_w2': _L0_xattn_in['w2'], 'L0_xattn_b2': _L0_xattn_in['b2'], 'L1_xattn_Wq': _L1_xattn_in['Wq'], 'L1_xattn_Wk': _L1_xattn_in['Wk'], 'L1_xattn_Wv': _L1_xattn_in['Wv'], 'L1_xattn_Wfc': _L1_xattn_in['Wfc'], 'L1_xattn_gamma': _L1_xattn_in['gamma'], 'L1_xattn_beta': _L1_xattn_in['beta']}

def reference(x, ctx_1024, L0_xattn_wq, L0_xattn_bq, L0_xattn_wk, L0_xattn_bk, L0_xattn_wv, L0_xattn_bv, L0_xattn_wo, L0_xattn_bo, L0_xattn_ln1_g, L0_xattn_ln1_b, L0_xattn_ln2_g, L0_xattn_ln2_b, L0_xattn_w1, L0_xattn_b1, L0_xattn_w2, L0_xattn_b2, L1_xattn_Wq, L1_xattn_Wk, L1_xattn_Wv, L1_xattn_Wfc, L1_xattn_gamma, L1_xattn_beta):
    import jax
    import jax.numpy as jnp

    def _L0_xattn_ref(query, key, value, wq, bq, wk, bk, wv, bv, wo, bo, ln1_g, ln1_b, ln2_g, ln2_b, w1, b1, w2, b2):
        import jax, jax.numpy as jnp
        import numpy as np
        E = 512
        H = 16
        HD = E // H
        EPS = 1e-05

        def _layer_norm(x, g, b):
            mu = jnp.mean(x, axis=-1, keepdims=True)
            var = jnp.var(x, axis=-1, keepdims=True)
            return (x - mu) * jax.lax.rsqrt(var + EPS) * g + b
        B, Sq, _ = query.shape
        Sk = key.shape[1]
        residual = query
        qn = _layer_norm(query, ln1_g, ln1_b)
        kn = _layer_norm(key, ln1_g, ln1_b)
        vn = _layer_norm(value, ln1_g, ln1_b)
        Q = (qn @ wq + bq).reshape(B, Sq, H, HD)
        K = (kn @ wk + bk).reshape(B, Sk, H, HD)
        V = (vn @ wv + bv).reshape(B, Sk, H, HD)
        scores = jnp.einsum('bqhd,bkhd->bhqk', Q, K) / jnp.sqrt(jnp.float32(HD))
        attn = jax.nn.softmax(scores, axis=-1)
        out = jnp.einsum('bhqk,bkhd->bqhd', attn, V).reshape(B, Sq, E)
        out = out @ wo + bo
        x = residual + out
        residual2 = x
        y = _layer_norm(x, ln2_g, ln2_b)
        y = jax.nn.gelu(y @ w1 + b1, approximate=False)
        y = y @ w2 + b2
        return residual2 + y

    def _L1_xattn_ref(q, k, v, Wq, Wk, Wv, Wfc, gamma, beta):
        import jax, jax.numpy as jnp
        import numpy as np
        B, S, D = (4, 1024, 512)
        H, DK, DV = (16, 64, 64)
        GRAPH_ATTN_BIAS = 2.0
        POS_WIN = 4.0
        LN_EPS = 1e-06
        b, sq, d = q.shape
        sk = k.shape[1]
        residual = q
        qh = (q @ Wq).reshape(b, sq, H, DK)
        kh = (k @ Wk).reshape(b, sk, H, DK)
        vh = (v @ Wv).reshape(b, sk, H, DV)
        attn = jnp.einsum('bqhd,bkhd->bhqk', qh / jnp.sqrt(jnp.float32(DK)), kh)
        gaussian_w = -0.5 * GRAPH_ATTN_BIAS ** 2 / (0.5 * POS_WIN) ** 2
        attn = attn + gaussian_w
        weights = jax.nn.softmax(attn, axis=-1)
        out = jnp.einsum('bhqk,bkhd->bqhd', weights, vh).reshape(b, sq, H * DV)
        out = out @ Wfc + residual
        mu = jnp.mean(out, axis=-1, keepdims=True)
        var = jnp.mean((out - mu) ** 2, axis=-1, keepdims=True)
        out = (out - mu) * jax.lax.rsqrt(var + LN_EPS) * gamma + beta
        return out
    x = _L0_xattn_ref(x, ctx_1024, ctx_1024, L0_xattn_wq, L0_xattn_bq, L0_xattn_wk, L0_xattn_bk, L0_xattn_wv, L0_xattn_bv, L0_xattn_wo, L0_xattn_bo, L0_xattn_ln1_g, L0_xattn_ln1_b, L0_xattn_ln2_g, L0_xattn_ln2_b, L0_xattn_w1, L0_xattn_b1, L0_xattn_w2, L0_xattn_b2)
    x = _L1_xattn_ref(x, ctx_1024, ctx_1024, L1_xattn_Wq, L1_xattn_Wk, L1_xattn_Wv, L1_xattn_Wfc, L1_xattn_gamma, L1_xattn_beta)
    return x

_drawn_inputs = setup_inputs


def setup_inputs(seed=0):
    import zlib

    import numpy as np

    out = dict(_drawn_inputs(seed))
    spreads = {'L0_xattn_bq': (0.0, 0.8),
     'L0_xattn_bk': (0.0, 0.8),
     'L0_xattn_bv': (0.0, 0.1),
     'L0_xattn_bo': (0.0, 0.1),
     'L0_xattn_ln1_g': (1.0, 0.6),
     'L0_xattn_ln1_b': (0.0, 0.405),
     'L0_xattn_ln2_g': (1.0, 0.2),
     'L0_xattn_ln2_b': (0.0, 0.345),
     'L0_xattn_b1': (0.0, 0.1),
     'L0_xattn_b2': (0.0, 0.1),
     'L1_xattn_gamma': (1.0, 0.2),
     'L1_xattn_beta': (0.0, 0.1)}
    factors = {'L0_xattn_wq': 7.437, 'L0_xattn_wk': 7.228, 'L1_xattn_Wq': 5.501, 'L1_xattn_Wk': 5.477}
    for name, (base, spread) in spreads.items():
        noise = np.random.default_rng([zlib.crc32(name.encode()), seed]).standard_normal(out[name].shape)
        drawn = base * np.exp(spread * noise) if base else spread * noise
        out[name] = jnp.asarray(drawn.astype(out[name].dtype))
    for name, factor in factors.items():
        out[name] = (out[name] * factor).astype(out[name].dtype)
    return out
```

```python
from contextlib import ExitStack

import concourse.bass as bass
from concourse import mybir

P = 128
B, SQ, SK, E = 8, 100, 722, 512
ROWS = B * SQ
ET = E // P
KT = -(-SK // P)
KROWS = [min(P, SK - P * t) for t in range(KT)]
HALF = SK // 2
RT = -(-ROWS // P)
RROWS = [min(P, ROWS - P * t) for t in range(RT)]
QHALF = ROWS // 2
H = 16
FF = 4 * E
FT = FF // P
WS = 256.0
HG = 4
MAX_T, PV_T = 4, 2

F32, F16 = mybir.dt.float32, mybir.dt.float16
ALU = mybir.AluOpType
ACT = mybir.ActivationFunctionType
AX = mybir.AxisListType
PARTS = ((0, 0), (0, 1), (1, 0))


class Scope:

    def __init__(self, nc, name):
        self.nc, self.name, self.stack, self.sems = nc, name, ExitStack(), []

    def __enter__(self):
        return self

    def __exit__(self, *a):
        self.stack.close()
        if self.sems:
            self.nc.clear_and_free_semaphores(self.sems)
            self.nc.all_engine_barrier()

    def sb(self, name, shape, dt=F32):
        return self.stack.enter_context(self.nc.sbuf_tensor(f"{self.name}_{name}", shape, dt))

    def ps(self, name, shape, dt=F32):
        return self.stack.enter_context(self.nc.psum_tensor(f"{self.name}_{name}", shape, dt))

    def sem(self, name):
        self.sems.append(self.nc.alloc_semaphore(f"{self.name}_{name}"))
        return self.sems[-1]

    def block(self):
        return self.stack.enter_context(self.nc.Block())


def make_constants(nc, ident, ident16, ones_mean, ones32):
    with Scope(nc, "const") as sc:
        zeroed, ident_made = sc.sem("zeroed"), sc.sem("ident_made")
        blk = sc.block()

        @blk.gpsimd
        def _(pool):
            pool.memset(ident[:], 0.0).then_inc(zeroed, 1)
            pool.wait_ge(zeroed, 1)
            pool.affine_select(out=ident[:], in_=ident[:], compare_op=ALU.not_equal, fill=1.0, base=0,
                               pattern=[[-1, P]], channel_multiplier=1).then_inc(ident_made, 1)

        @blk.vector
        def _(dve):
            dve.memset(ones_mean[:], 1.0 / E)
            dve.memset(ones32[:], 1.0)
            dve.wait_ge(ident_made, 1)
            dve.tensor_copy(ident16[:], ident[:])


def split_weights(nc, name, jobs):
    with Scope(nc, name) as sc:
        w32 = sc.sb("w32", [P, 2, ET, E])
        loaded = [sc.sem(f"loaded{i}") for i in range(2)]
        hi_made, lo_made = sc.sem("hi_made"), sc.sem("lo_made")
        blk = sc.block()

        @blk.sync
        def _(sp):
            for n, (src, _hi, _lo) in enumerate(jobs):
                if n >= 2:
                    sp.wait_ge(lo_made, n - 1)
                sp.dma_start(w32[:, n % 2], src).then_inc(loaded[n % 2], 16)

        @blk.scalar
        def _(act):
            for n, (_src, hi, _lo) in enumerate(jobs):
                act.wait_ge(loaded[n % 2], 16 * (n // 2 + 1))
                act.activation(hi, w32[:, n % 2], ACT.Identity, scale=WS).then_inc(hi_made, 1)

        @blk.vector
        def _(dve):
            for n, (_src, hi, lo) in enumerate(jobs):
                dve.wait_ge(hi_made, n + 1)
                dve.scalar_tensor_tensor(lo, w32[:, n % 2], WS, hi, ALU.mult, ALU.subtract).then_inc(lo_made, 1)


def fold_norm_weights(nc, wk_d, wv_d, g_col, b_col, bk_col, bv_row, ones_mean, wk, wv, kb_col, vb_row):
    with Scope(nc, "fold") as sc:
        w32 = sc.sb("w32", [P, 2, ET, E])
        wg = sc.sb("wg", [P, 2, ET, E])
        b_wide = sc.sb("b_wide", [P, ET, P])
        pk = sc.ps("pk", [P, 512])
        pv = sc.ps("pv", [P, 512])
        pmean = sc.ps("pmean", [P, 2, 512])
        loaded = [sc.sem(f"loaded{i}") for i in range(2)]
        b_widened, scaled, bias_ready, mean_ready = (sc.sem(n) for n in ("b_widened", "scaled", "bias_ready", "mean_ready"))
        centred, hi_made = sc.sem("centred"), sc.sem("hi_made")
        blk = sc.block()

        @blk.sync
        def _(sp):
            for n, src in enumerate((wk_d, wv_d)):
                sp.dma_start(w32[:, n], src.rearrange("(k p) n -> p k n", p=P)).then_inc(loaded[n], 16)

        @blk.vector
        def _(dve):
            for k in range(ET):
                dve.tensor_copy(b_wide[:, k, :], b_col[:, k:k + 1].to_broadcast([P, P])).then_inc(b_widened, 1)
            for n in range(2):
                dve.wait_ge(loaded[n], 16)
                for k in range(ET):
                    dve.tensor_scalar(wg[:, n, k, :], w32[:, n, k, :], g_col[:, k:k + 1], None, ALU.mult).then_inc(scaled, 1)
            dve.wait_ge(bias_ready, 2)
            dve.tensor_tensor(kb_col[:], pk[:, 0:ET], bk_col[:], ALU.add)
            dve.tensor_tensor(vb_row[:], pv[:], bv_row[:], ALU.add)
            for n in range(2):
                dve.wait_ge(mean_ready, n + 1)
                for k in range(ET):
                    dve.tensor_tensor(w32[:, n, k, :], wg[:, n, k, :], pmean[:, n, :], ALU.subtract).then_inc(centred, 1)
            for n, w in enumerate((wk, wv)):
                dve.wait_ge(hi_made, n + 1)
                dve.scalar_tensor_tensor(w[:, 1], w32[:, n], WS, w[:, 0], ALU.mult, ALU.subtract)

        @blk.tensor
        def _(pe):
            pe.wait_ge(b_widened, ET)
            pe.wait_ge(loaded[0], 16)
            for m in range(ET):
                for k in range(ET):
                    last = pe.matmul(pk[:, m:m + 1], w32[:, 0, k, m * P:(m + 1) * P], b_col[:, k:k + 1],
                                     start=(k == 0), stop=(k == ET - 1))
            last.then_inc(bias_ready, 1)
            pe.wait_ge(loaded[1], 16)
            for k in range(ET):
                last = pe.matmul(pv[:], b_wide[:, k, :], w32[:, 1, k, :], start=(k == 0), stop=(k == ET - 1))
            last.then_inc(bias_ready, 1)
            for n in range(2):
                pe.wait_ge(scaled, ET * (n + 1))
                for k in range(ET):
                    last = pe.matmul(pmean[:, n, :], ones_mean[:], wg[:, n, k, :], start=(k == 0), stop=(k == ET - 1))
                last.then_inc(mean_ready, 1)

        @blk.scalar
        def _(act):
            for n, w in enumerate((wk, wv)):
                act.wait_ge(centred, ET * (n + 1))
                act.activation(w[:, 0], w32[:, n], ACT.Identity, scale=WS).then_inc(hi_made, 1)


def rows_stage(nc, name, ident16, res_d, w=None, lhs=None, res=None, bias=None, norm=None, keep=None, store=None, xT=None):
    kt = lhs.shape[2] if lhs is not None else 0
    with Scope(nc, name) as sc:
        if res is None:
            res = sc.sb("res", [P, RT, E])
        y = keep if keep is not None else (sc.sb("y", [P, RT, E]) if w is not None else res)
        z = sc.sb("z", [P, RT, E]) if norm else y
        hi = sc.sb("hi", [P, RT, E], F16)
        lo = sc.sb("lo", [P, RT, E], F16)
        stats = sc.sb("stats", [P, RT, 6])
        mv = sc.sb("mv", [P, RT, 2])
        rstd = sc.sb("rstd", [P, RT])
        half_power = sc.sb("half_power", [P, 1])
        power_set, var_made = sc.sem("power_set"), sc.sem("var_made")
        acc = sc.ps("acc", [P, 4, 512])
        tr = [sc.ps(f"tr{i}", [P, 2, ET, P], F16) for i in range(2)]
        loaded = [sc.sem(f"loaded{t}") for t in range(RT)]
        names = ("acc_ready", "summed", "biased", "stats_made", "mv_made", "rstd_made", "normed", "scaled",
                 "affined", "hi_made", "lo_made", "tr_ready", "tr_freed", "stored")
        (acc_ready, summed, biased, stats_made, mv_made, rstd_made, normed, scaled, affined, hi_made, lo_made,
         tr_ready, tr_freed, stored) = (sc.sem(n) for n in names)
        blk = sc.block()

        def wait_y(eng, T):
            if bias is not None:
                eng.wait_ge(biased, T + 1)
            elif w is not None:
                eng.wait_ge(summed, T + 1)
            else:
                eng.wait_ge(loaded[T], 16)

        def wait_z(eng, T):
            if norm:
                eng.wait_ge(affined, T + 1)
            else:
                wait_y(eng, T)

        @blk.sync
        def _(sp):
            if res_d is not None:
                for T, r in enumerate(RROWS):
                    sp.dma_start(res[:r, T], res_d[P * T:P * T + r, :]).then_inc(loaded[T], 16)
            if store is not None:
                for T, r in enumerate(RROWS):
                    wait_z(sp, T)
                    sp.dma_start(store[P * T:P * T + r, :], z[:r, T]).then_inc(stored, 16)
                sp.wait_ge(stored, 16 * RT)

        @blk.tensor
        def _(pe):
            for i in range(RT + 2):
                if i < RT and w is not None:
                    r = RROWS[i]
                    if i >= 4:
                        pe.wait_ge(summed, i - 3)
                    n = 0
                    for k in range(kt):
                        for a, b in PARTS:
                            last = pe.matmul(acc[:r, i % 4, :], lhs[:, a, k, P * i:P * i + r], w[:, b, k, :],
                                             start=(n == 0), stop=(n == 3 * kt - 1))
                            n += 1
                    last.then_inc(acc_ready, 1)
                T = i - 2
                if T >= 0 and xT is not None:
                    r = RROWS[T]
                    pe.wait_ge(lo_made, T + 1)
                    if T >= 2:
                        pe.wait_ge(tr_freed, T - 1)
                    for a, part in enumerate((hi, lo)):
                        for k in range(ET):
                            last = pe.transpose(tr[T % 2][:, a, k, :r], part[:r, T, k * P:(k + 1) * P], ident16[:r, :r])
                    last.then_inc(tr_ready, 1)

        @blk.vector
        def _(dve):
            for i in range(RT + 2):
                if i < RT:
                    T, r = i, RROWS[i]
                    if w is not None:
                        dve.wait_ge(acc_ready, T + 1)
                        if res_d is not None:
                            dve.wait_ge(loaded[T], 16)
                        dve.scalar_tensor_tensor(y[:r, T], acc[:r, T % 4, :], 1.0 / WS, res[:r, T], ALU.mult,
                                                 ALU.add).then_inc(summed, 1)
                T = i - 1
                if 0 <= T < RT and norm:
                    r = RROWS[T]
                    wait_y(dve, T)
                    dve.bn_stats(stats[:r, T, :], y[:r, T]).then_inc(stats_made, 1)
                    dve.wait_ge(stats_made, T + 1)
                    dve.bn_aggr(mv[:r, T, :], stats[:r, T, :]).then_inc(mv_made, 1)
                    dve.wait_ge(rstd_made, T + 1)
                    dve.tensor_scalar(z[:r, T], y[:r, T], mv[:r, T, 0:1], rstd[:r, T:T + 1], ALU.subtract,
                                      ALU.mult).then_inc(normed, 1)
                T = i - 2
                if T >= 0 and xT is not None:
                    r = RROWS[T]
                    dve.wait_ge(hi_made, T + 1)
                    dve.tensor_tensor(lo[:r, T], z[:r, T], hi[:r, T], ALU.subtract).then_inc(lo_made, 1)
                    dve.wait_ge(tr_ready, T + 1)
                    dve.tensor_copy(xT[:, :, :, P * T:P * T + r], tr[T % 2][:, :, :, :r]).then_inc(tr_freed, 1)

        @blk.gpsimd
        def _(pool):
            pool.memset(half_power[:], -0.5).then_inc(power_set, 1)
            pool.wait_ge(power_set, 1)
            for i in range(RT + 1):
                if i < RT and bias is not None:
                    r = RROWS[i]
                    pool.wait_ge(summed, i + 1)
                    pool.tensor_tensor(y[:r, i], y[:r, i], bias[:r], ALU.add).then_inc(biased, 1)
                T = i - 1
                if T >= 0 and norm:
                    eps, g_row, b_row = norm
                    r = RROWS[T]
                    pool.wait_ge(mv_made, T + 1)
                    pool.tensor_scalar(rstd[:r, T:T + 1], mv[:r, T, 1:2], eps, None, ALU.add).then_inc(var_made, 1)
                    pool.wait_ge(var_made, T + 1)
                    pool.tensor_tensor(rstd[:r, T:T + 1], rstd[:r, T:T + 1], half_power[:r, :], ALU.pow).then_inc(rstd_made, 1)
                    pool.wait_ge(normed, T + 1)
                    pool.tensor_tensor(z[:r, T], z[:r, T], g_row[:r], ALU.mult).then_inc(scaled, 1)
                    pool.wait_ge(scaled, T + 1)
                    pool.tensor_tensor(z[:r, T], z[:r, T], b_row[:r], ALU.add).then_inc(affined, 1)

        @blk.scalar
        def _(act):
            if xT is not None:
                for T, r in enumerate(RROWS):
                    wait_z(act, T)
                    act.copy(hi[:r, T], z[:r, T]).then_inc(hi_made, 1)


def columns_stage(nc, name, xT, w, m_tiles, func, bias_col, scale, outT, store=None):
    kt = xT.shape[2]
    with Scope(nc, name) as sc:
        out32 = sc.sb("out32", [P, 3, QHALF])
        acc = sc.ps("acc", [P, 4, 512])
        acc_ready, made, hi_made, lo_made, stored = (sc.sem(n) for n in ("acc_ready", "made", "hi_made", "lo_made", "stored"))
        blk = sc.block()
        uses = [(m, n) for m in range(m_tiles) for n in range(2)]

        @blk.tensor
        def _(pe):
            for u, (m, n) in enumerate(uses):
                if u >= 4:
                    pe.wait_ge(made, u - 3)
                j = 0
                for k in range(kt):
                    for a, b in PARTS:
                        last = pe.matmul(acc[:, u % 4, :QHALF], w[:, a, k, m * P:(m + 1) * P],
                                         xT[:, b, k, n * QHALF:(n + 1) * QHALF], start=(j == 0), stop=(j == 3 * kt - 1))
                        j += 1
                last.then_inc(acc_ready, 1)

        @blk.scalar
        def _(act):
            for u, (m, n) in enumerate(uses):
                act.wait_ge(acc_ready, u + 1)
                if u >= 3:
                    act.wait_ge(lo_made, u - 2)
                bias = bias_col[:, m:m + 1] if bias_col is not None else 0.0
                act.activation(out32[:, u % 3, :], acc[:, u % 4, :QHALF], func, bias=bias, scale=scale).then_inc(made, 1)

        @blk.vector
        def _(dve):
            for u, (m, n) in enumerate(uses):
                cols = slice(n * QHALF, (n + 1) * QHALF)
                dve.wait_ge(made, u + 1)
                dve.tensor_copy(outT[:, 0, m, cols], out32[:, u % 3, :]).then_inc(hi_made, 1)
                dve.wait_ge(hi_made, u + 1)
                dve.tensor_tensor(outT[:, 1, m, cols], out32[:, u % 3, :], outT[:, 0, m, cols], ALU.subtract).then_inc(lo_made, 1)

        @blk.sync
        def _(sp):
            if store is not None:
                sp.wait_ge(lo_made, len(uses))
                for a in range(2):
                    sp.dma_start(store[a], outT[:, a]).then_inc(stored, 16)
                sp.wait_ge(stored, 32)


class Slots:

    def __init__(self, layer):
        self.layer = layer
        self.groups = 4 if layer == 0 else 2
        self.n = KT * self.groups
        self.heads = HG * self.groups
        at = [0, 1, 3, 4, 6, 7, 9, 10, 12, 13, 15, 16, 19, 22] if layer == 0 else [0, 0, 1, 1, 2, 2, 3, 3, 4, 6, 7, 8, 10, 11]
        self.proj = [[a for a in range(14) if at[a] == j] for j in range(self.n)]
        self.evac = [(self.proj[j - 1][-1:] if j else []) + self.proj[j][:-1] for j in range(self.n)]
        self.evac[-1] = self.evac[-1] + self.proj[-1][-1:]
        self.k_lo = {j + 1: a // 2 for j in range(self.n) for a in self.evac[j] if a < 8 and a % 2}
        self.ctx = {2: 0, 5: 1, 8: 2, 11: 3, 14: 4, 17: 5} if layer == 0 else {}
        self.var_t, self.diag_t = 17, 19
        self.bc = {20: 0, 21: 1} if layer == 0 else {}
        self.out_t = 9
        self.units = B if layer == 0 else 2 * B

    def misc(self, prep, proj, scores, outs):
        uses = []
        for j in range(self.n):
            g, t = divmod(j, KT)
            if prep and j in self.ctx:
                uses.append(("ctx", self.ctx[j]))
            if prep and j in self.bc:
                uses.append(("bc", self.bc[j]))
            if outs and j == self.out_t:
                uses.append(("out", 0))
            if t == MAX_T and (scores if g < self.groups - 1 else proj):
                uses.append(("max", g))
        return uses

    def kind(self, s):
        return (self.layer == 0 and s + 1 < self.units, s < self.units, 1 <= s <= self.units, s >= 2)

    def misc_count(self, s, use):
        before = KT + 2 if self.layer == 0 else 0
        if isinstance(s, int):
            if s < 0:
                return ([("ctx", t) for t in range(KT)] + [("bc", 0), ("bc", 1)]).index(use) + 1
            for q in range(s):
                before += len(self.misc(*self.kind(q)))
            return before + self.misc(*self.kind(s)).index(use) + 1
        for q in range(2):
            before += len(self.misc(*self.kind(q)))
        steady = self.misc(*self.kind(2))
        return (s - 2) * len(steady) + (before + steady.index(use) + 1)


def attention(nc, layer, ctx_d, ctxT_d, q_d, w_k, w_v, kb_col, vb_row, ident, ident16, ones32, eps, score_bias, outT):
    sl = Slots(layer)
    NG, NH, U = sl.groups, sl.heads, sl.units
    DK = 32 if layer == 0 else 64
    HPT = P // DK
    MR = 96 if layer == 0 else 64
    VC = 2 * DK + 1
    OC = VC if layer == 0 else DK + 1
    NPROJ = 14
    NSTACK = 3 * HPT
    NQ = 3 * HPT
    NSLOT = sl.n
    PW = HG * SQ + (P - SQ)

    with Scope(nc, f"attn{layer}") as sc:
        ctxT = sc.sb("ctxT", [P, 2, 2, ET, SK], F16)
        knat = sc.sb("knat", [P, 2, 2, SK], F16)
        if layer == 0:
            kstack = [sc.sb("kstack", [P, 2, NH, SK], F16)]
            qstack = [sc.sb("qstack", [P, 2, NH, SQ], F16)]
        else:
            kstack = [sc.sb("kstack_a", [P, 2, NH, SK], F16), sc.sb("kstack_b", [P, 2, NH, SK], F16)]
            qstack = [sc.sb("qstack_a", [P, 2, NH, SQ], F16), sc.sb("qstack_b", [P, 2, NH, SQ], F16)]
        vbuf = sc.sb("vbuf", [P, 2, KT, NH, VC], F16)
        p32 = sc.sb("p32", [P, 3, HG * SQ])
        probs = sc.sb("probs", [P, 2, 2, KT, PW], F16)
        onehot = sc.sb("onehot", [P, HG], F16)
        nmax = sc.sb("nmax", [P, HG])
        nmax_parts = sc.sb("nmax_parts", [P, P], F16)
        pv_sb = sc.sb("pv_sb", [P, 2, HG, OC])
        osum = sc.sb("osum", [P, HG, DK])
        orecip = sc.sb("orecip", [P, 2, HG])
        o32 = sc.sb("o32", [P, E])
        oparts = sc.sb("oparts", [P, 2, E], F16)
        if layer == 0:
            c32 = sc.sb("c32", [P, 3, E])
            cparts = sc.sb("cparts", [P, 2, 2, E], F16)
            stats = sc.sb("stats", [P, 3, 6])
            mv = sc.sb("mv", [P, KT, 2])
            var = sc.sb("var", [P, KT])
            half_power = sc.sb("half_power", [P, KT])
            rstd = sc.sb("rstd", [P, 2, KT])
            rdiag = sc.sb("rdiag", [P, KT, P])
            rrow = sc.sb("rrow", [P, 2, SK])
            kscaled = sc.sb("kscaled", [P, 2, SK])
        p_proj = sc.ps("p_proj", [P, 2, 512])
        p_max = sc.ps("p_max", [P, 2, 512])
        p_sc = sc.ps("p_sc", [P, 2, 512])
        p_pv = sc.ps("p_pv", [P, 512])
        misc32 = sc.ps("misc", [P, 512])
        misc16 = misc32[:].bitcast(F16)

        padded, onehot_made, onehot_seeded, onehot_placed = (sc.sem(n) for n in (
            "padded", "onehot_made", "onehot_seeded", "onehot_placed"))
        bias_col = sc.sb("score_bias", [P, 1])
        (proj_ready, proj_freed, k_hi_made, k_lo_made, v_hi_made, max_ready, max_made, nm_hi_made, nm_made,
         misc_ready, misc_freed, sc_ready, exp_made, p_hi_made, pv_ready, pv_copied, recip_made,
         o_summed, o_normed, o_made, o_hi_made, o_lo_made) = (sc.sem(n) for n in (
             "proj_ready", "proj_freed", "k_hi_made", "k_lo_made", "v_hi_made", "max_ready", "max_made",
             "nm_hi_made", "nm_made", "misc_ready", "misc_freed", "sc_ready", "exp_made", "p_hi_made",
             "pv_ready", "pv_copied", "recip_made", "o_summed", "o_normed", "o_made",
             "o_hi_made", "o_lo_made"))
        p_lo_made = [sc.sem(f"p_lo_made{i}") for i in range(2)]
        stacked = [sc.sem(f"stacked{m}") for m in range(4)]
        q_loaded = [sc.sem(f"q_loaded{i}") for i in range(2)]
        ctxT_moved = [sc.sem(f"ctxT_moved{i}") for i in range(2)]
        if layer == 0:
            c_loaded = [sc.sem(f"c_loaded{i}") for i in range(3)]
            (c_hi_made, c_lo_made, stats_made, mv_made, var_made, rstd_made, rdiag_made) = (sc.sem(n) for n in (
                "c_hi_made", "c_lo_made", "stats_made", "mv_made", "var_made", "rstd_made", "rdiag_made"))
        blk = sc.block()

        def lo_count(u, g, t):
            return (u * NG + g) * (KT // 2) + (t // 2 + 1)

        def prob_lo(eng, u, g, t):
            r = KROWS[t]
            eng.wait_ge(p_hi_made, (u * NG + g) * KT + (t + 1))
            eng.tensor_tensor(probs[:r, g % 2, 1, t, :HG * SQ], p32[:r, t % 3, :], probs[:r, g % 2, 0, t, :HG * SQ],
                              ALU.subtract).then_inc(p_lo_made[t % 2], 1)

        def steps(eng, step):
            last_loop = U - 2 if layer == 0 else U
            for s in range(2):
                step(s, s % 2, sl.kind(s))
            with eng.Fori(1, last_loop // 2) as i:
                for par in range(2):
                    step(2 * i + par, par, sl.kind(2))
            for s in range(last_loop, U + 2):
                step(s, s % 2, sl.kind(s))

        @blk.sync
        def _(sp):
            def load_ctx_tile(b, t):
                if not (isinstance(b, int) and b * KT + t < 3):
                    sp.wait_ge(c_hi_made, b * KT + (t - 2))
                    sp.wait_ge(c_lo_made, b * KT + (t - 2))
                    sp.wait_ge(stats_made, b * KT + (t - 2))
                r = KROWS[t]
                sp.dma_start(c32[:r, t % 3, :], ctx_d[bass.ds(b, 1), P * t:P * t + r, :].rearrange("o p e -> (o p) e")
                             ).then_inc(c_loaded[t % 3], 16)

            def spill_ctx(b, par):
                sp.wait_ge(misc_freed, sl.misc_count(b - 1, ("ctx", KT - 1)))
                sp.dma_start(ctxT_d[bass.ds(b, 1)].rearrange("o p n -> (o p) n"), ctxT[:, par].rearrange("p a k s -> p (a k s)")
                             ).then_inc(ctxT_moved[par], 16)

            def load_ctxT(u, par, b):
                if not (isinstance(u, int) and u < 2):
                    sp.wait_ge(proj_ready, NPROJ * (u - 1))
                sp.dma_start(ctxT[:, par].rearrange("p a k s -> p (a k s)"), ctxT_d[bass.ds(b, 1)].rearrange("o p n -> (o p) n")
                             ).then_inc(ctxT_moved[par], 16)

            def load_q(u, par, b):
                if not (isinstance(u, int) and u < 2):
                    sp.wait_ge(sc_ready, NSLOT * (u - 1))
                for j in range(HPT):
                    for row, a in enumerate((0, 0, 1)):
                        dst = qstack[0] if layer == 0 or row < 2 else qstack[1]
                        row0 = DK * row if layer == 0 or row < 2 else 0
                        m0 = 0 if layer == 0 else 4 * par
                        sp.dma_start(dst[row0:row0 + DK, par].rearrange("p (m j) q -> p m j q", j=HPT)[:, :, j, :],
                                     q_d[a, DK * j:DK * j + DK, m0:m0 + 4, bass.ds(b * SQ, SQ)]).then_inc(q_loaded[par], 16)

            def stack_k(u, par, m):
                if layer == 0:
                    sp.wait_ge(k_lo_made, 4 * u + (m + 1))
                else:
                    sp.wait_ge(proj_freed, NPROJ * u + (2 * m + 2))
                for j in range(HPT):
                    for row, a in enumerate((0, 1, 0)):
                        dst = kstack[0] if layer == 0 or row < 2 else kstack[1]
                        row0 = DK * row if layer == 0 or row < 2 else 0
                        sp.dma_start(dst[row0:row0 + DK, par, HPT * m + j, :],
                                     knat[DK * j:DK * j + DK, m % 2, a, :]).then_inc(stacked[m], 16)

            def place_onehot():
                sp.wait_ge(onehot_seeded, HG)
                rows = kstack[-1][MR:MR + 2 * HG]
                for par in range(2):
                    for g in range(NG):
                        if par or g:
                            sp.dma_start(rows[:, par, HG * g:HG * g + HG, :], rows[:, 0, 0:HG, :]).then_inc(onehot_placed, 16)

            if layer == 0:
                def step(s, par, kind):
                    prep, proj, _scores, _outs = kind
                    if prep:
                        for t in range(3):
                            load_ctx_tile(s + 1, t)
                    if proj:
                        load_q(s, par, s)
                    for m in range(4):
                        if proj:
                            stack_k(s, par, m)
                        if prep and m < 3:
                            load_ctx_tile(s + 1, 3 + m)
                    if prep:
                        spill_ctx(s + 1, 1 - par)

                for t in range(KT):
                    load_ctx_tile(0, t)
                place_onehot()
                spill_ctx(0, 0)
                steps(sp, step)
                for i in range(2):
                    sp.wait_ge(ctxT_moved[i], 16 * (B // 2))
            else:
                def unit(u, par, b, ahead=True):
                    load_q(u, par, b)
                    for m in range(4):
                        stack_k(u, par, m)
                    if ahead:
                        load_ctxT(u + 2, par, b + 1)

                load_ctxT(0, 0, 0)
                load_ctxT(1, 1, 0)
                place_onehot()
                for u in range(2):
                    unit(u, u, 0)
                with sp.Fori(1, B - 1) as b:
                    for par in range(2):
                        unit(2 * b + par, par, b)
                for u in range(U - 2, U):
                    unit(u, u % 2, B - 1, ahead=False)

        @blk.tensor
        def _(pe):
            def misc_wait(s, use, first=False):
                if not first:
                    pe.wait_ge(misc_freed, sl.misc_count(s, use) - 1)

            def ctx_transposes(s, par, t):
                b, r = s + 1, KROWS[t]
                pe.wait_ge(c_hi_made, b * KT + (t + 1))
                pe.wait_ge(c_lo_made, b * KT + (t + 1))
                misc_wait(s, ("ctx", t), first=(isinstance(s, int) and s < 0 and t == 0))
                for a in range(2):
                    for k in range(ET):
                        o = (a * ET + k) * P
                        last = pe.transpose(misc16[:, o:o + r], cparts[:r, t % 2, a, k * P:(k + 1) * P], ident16[:r, :r])
                last.then_inc(misc_ready, 1)

            def rstd_rows(s, n):
                pe.wait_ge(rdiag_made, (s + 2) * KT)
                misc_wait(s, ("bc", n))
                for t in range(3 * n, 3 * n + 3):
                    r = KROWS[t]
                    o = P * (t - 3 * n)
                    last = pe.matmul(misc32[:, o:o + r], ones32[:r, :], rdiag[:r, t, :r], start=True, stop=True)
                last.then_inc(misc_ready, 1)

            def project(u, par, a):
                n_use = NPROJ * u + a
                if not (isinstance(u, int) and n_use < 2):
                    pe.wait_ge(proj_freed, NPROJ * u + (a - 1))
                if a == 0:
                    if layer == 1:
                        pe.wait_ge(ctxT_moved[par], 16 * (u // 2 + 1) if isinstance(u, int) else 8 * (u - par) + 16)
                    else:
                        pe.wait_ge(misc_freed, sl.misc_count(u - 1, ("ctx", KT - 1)))
                c0 = 0 if layer == 0 else E * par
                bank = p_proj[:, a % 2, :]
                j = 0
                for k in range(ET):
                    for wa, ca in PARTS:
                        flags = dict(start=(j == 0), stop=(j == 3 * ET - 1))
                        if a < 8:
                            m, n = divmod(a, 2)
                            last = pe.matmul(bank[:, :HALF], w_k[:, wa, k, c0 + m * P:c0 + (m + 1) * P],
                                             ctxT[:, par, ca, k, n * HALF:(n + 1) * HALF], **flags)
                        else:
                            t = a - 8
                            r = KROWS[t]
                            last = pe.matmul(bank[:r, :], ctxT[:, par, ca, k, P * t:P * t + r],
                                             w_v[:, wa, k, c0:c0 + E], **flags)
                        j += 1
                last.then_inc(proj_ready, 1)

            def max_scores(u, par, g, hh):
                n_use = (u * NG + g) * HG + hh
                h = HG * g + hh
                if hh == 0 and g == 0:
                    pe.wait_ge(q_loaded[par], 16 * NQ * (u // 2 + 1) if isinstance(u, int) else 8 * NQ * (u - par) + 16 * NQ)
                if h % HPT == 0:
                    pe.wait_ge(stacked[h // HPT], 16 * NSTACK * (u + 1))
                if not (isinstance(u, int) and n_use < 1):
                    pe.wait_ge(max_made, n_use)
                kr = MR if layer == 0 else P
                for n in range(2):
                    last = pe.matmul(p_max[:SQ, n, :HALF], qstack[0][:kr, par, h, :],
                                     kstack[0][:kr, par, h, n * HALF:(n + 1) * HALF], start=True, stop=True)
                last.then_inc(max_ready, 1)

            def max_transposes(s, G1, g):
                pe.wait_ge(nm_made, G1)
                misc_wait(s, ("max", g), first=(layer == 1 and isinstance(s, int) and s == 0))
                pe.transpose(misc16[:, :SQ], nmax_parts[:SQ, :], ident16[:SQ, :SQ]).then_inc(misc_ready, 1)

            def scores(s, u, par, g, t):
                n_use = (u * NG + g) * KT + t
                r = KROWS[t]
                if g == 0 and t == 0 and isinstance(u, int) and u == 0:
                    pe.wait_ge(onehot_placed, 16 * (2 * NG - 1))
                if t == 0:
                    pe.wait_ge(misc_freed, sl.misc_count(s, ("max", g - 1)) if g else sl.misc_count(s - 1, ("max", NG - 1)))
                if not (isinstance(u, int) and n_use < 2):
                    pe.wait_ge(exp_made, n_use - 1)
                for hh in range(HG):
                    h = HG * g + hh
                    out = p_sc[:r, t % 2, hh * SQ:(hh + 1) * SQ]
                    if layer == 0:
                        last = pe.matmul(out, kstack[0][:MR + 2 * HG, par, h, P * t:P * t + r],
                                         qstack[0][:MR + 2 * HG, par, h, :], start=True, stop=True)
                    else:
                        pe.matmul(out, kstack[0][:, par, h, P * t:P * t + r], qstack[0][:, par, h, :], start=True, stop=False)
                        last = pe.matmul(out, kstack[1][:MR + 2 * HG, par, h, P * t:P * t + r],
                                         qstack[1][:MR + 2 * HG, par, h, :], start=False, stop=True)
                last.then_inc(sc_ready, 1)

            def times_v(u, par, g, hh):
                G = u * NG + g
                if hh == 0:
                    for i in range(2):
                        pe.wait_ge(p_lo_made[i], (G + 1) * (KT // 2))
                    if g == 0:
                        pe.wait_ge(proj_freed, NPROJ * (u + 1))
                    if not (isinstance(u, int) and G == 0):
                        pe.wait_ge(pv_copied, G)
                h = HG * g + hh
                o = hh * OC
                for t in range(KT):
                    r = KROWS[t]
                    v = vbuf[:r, par, t, h, :]
                    ph, pl = (probs[:r, g % 2, a, t, hh * SQ:hh * SQ + P] for a in range(2))
                    first, end = t == 0, t == KT - 1
                    if layer == 0:
                        pe.matmul(p_pv[:, o:o + OC], ph, v, start=first, stop=False)
                        last = pe.matmul(p_pv[:, o:o + OC], pl, v, start=False, stop=end)
                    else:
                        pe.matmul(p_pv[:, o:o + OC], ph, v[:, :OC], start=first, stop=False)
                        pe.matmul(p_pv[:, o:o + DK], ph, v[:, OC:], start=False, stop=False)
                        last = pe.matmul(p_pv[:, o:o + OC], pl, v[:, :OC], start=False, stop=end)
                if hh == HG - 1:
                    last.then_inc(pv_ready, 1)

            def out_transposes(s):
                pe.wait_ge(o_lo_made, s - 1)
                misc_wait(s, ("out", 0))
                for a in range(2):
                    for k in range(ET):
                        o = (a * ET + k) * P
                        last = pe.transpose(misc16[:, o:o + SQ], oparts[:SQ, a, k * P:(k + 1) * P], ident16[:SQ, :SQ])
                last.then_inc(misc_ready, 1)

            def step(s, par, kind):
                prep, proj, has_scores, outs = kind
                for j in range(sl.n):
                    g, t = divmod(j, KT)
                    if has_scores:
                        scores(s, s - 1, 1 - par, g, t)
                    if prep and j in sl.ctx:
                        ctx_transposes(s, par, sl.ctx[j])
                    if prep and j in sl.bc:
                        rstd_rows(s, sl.bc[j])
                    if outs and j == sl.out_t:
                        out_transposes(s)
                    if g < NG - 1:
                        if has_scores and t < HG:
                            max_scores(s - 1, 1 - par, g + 1, t)
                        if has_scores and t == MAX_T:
                            max_transposes(s, (s - 1) * NG + (g + 2), g)
                    elif proj:
                        if t < HG:
                            max_scores(s, par, 0, t)
                        if t == MAX_T:
                            max_transposes(s, s * NG + 1, g)
                    if 0 <= t - PV_T < HG:
                        if g == 0 and outs:
                            times_v(s - 2, par, NG - 1, t - PV_T)
                        if g > 0 and has_scores:
                            times_v(s - 1, 1 - par, g - 1, t - PV_T)
                    if proj:
                        for a in sl.proj[j]:
                            project(s, par, a)

            if layer == 0:
                for t in range(KT):
                    ctx_transposes(-1, 1, t)
                for n in range(2):
                    rstd_rows(-1, n)
            steps(pe, step)

        @blk.scalar
        def _(act):
            def ctx_hi(b, t):
                r = KROWS[t]
                act.wait_ge(c_loaded[t % 3], 32 * b + 16 * (t // 3 + 1))
                if not (isinstance(b, int) and b == 0 and t < 2):
                    act.wait_ge(misc_ready, sl.misc_count(b - 1, ("ctx", t - 2)) if t >= 2 else sl.misc_count(b - 2, ("ctx", KT - 2 + t)))
                act.copy(cparts[:r, t % 2, 0, :], c32[:r, t % 3, :]).then_inc(c_hi_made, 1)

            def rstd_row(s, par, n):
                act.wait_ge(misc_ready, sl.misc_count(s, ("bc", n)))
                c = slice(0, 3 * P) if n == 0 else slice(3 * P, SK)
                act.copy(rrow[:, 1 - par, c], misc32[:, :c.stop - c.start]).then_inc(misc_freed, 1)

            def exp(u, g, t):
                n_use = (u * NG + g) * KT + t
                r = KROWS[t]
                act.wait_ge(sc_ready, n_use + 1)
                if not (isinstance(u, int) and n_use < 3):
                    act.wait_ge(p_lo_made[1 - t % 2], lo_count(u, g, t - 3))
                act.activation(p32[:r, t % 3, :], p_sc[:r, t % 2, :HG * SQ], ACT.Exp,
                               bias=bias_col[:r, 0:1] if score_bias else 0.0).then_inc(exp_made, 1)

            def prob_hi(u, g, t):
                n_use = (u * NG + g) * KT + t
                r = KROWS[t]
                act.wait_ge(exp_made, n_use + 1)
                G = u * NG + g
                if t == 0 and not (isinstance(u, int) and G < 2):
                    act.wait_ge(pv_ready, G - 1)
                act.copy(probs[:r, g % 2, 0, t, :HG * SQ], p32[:r, t % 3, :]).then_inc(p_hi_made, 1)

            def evacuate(u, par, a):
                if a < 8:
                    m, n = divmod(a, 2)
                    if layer == 0:
                        if n == 0:
                            return
                        act.wait_ge(proj_freed, NPROJ * u + (a + 1))
                        cols = slice(0, SK)
                        src = kscaled[:, m % 2, :]
                    else:
                        act.wait_ge(proj_ready, NPROJ * u + (a + 1))
                        cols = slice(n * HALF, (n + 1) * HALF)
                        src = p_proj[:, a % 2, :HALF]
                    if n == 0 or layer == 0:
                        if m >= 2:
                            act.wait_ge(stacked[m - 2], 16 * NSTACK * (u + 1))
                        elif not (isinstance(u, int) and u == 0):
                            act.wait_ge(stacked[m + 2], 16 * NSTACK * u)
                    if layer == 0:
                        act.activation(knat[:, m % 2, 0, cols], src, ACT.Identity, bias=kb_col[:, m:m + 1]).then_inc(k_hi_made, 1)
                    else:
                        act.activation(knat[:, m % 2, 0, cols], src, ACT.Identity, scale=1.0 / WS).then_inc(k_hi_made, 1)
                else:
                    t = a - 8
                    r = KROWS[t]
                    act.wait_ge(proj_ready, NPROJ * u + (a + 1))
                    if t == 0 and not (isinstance(u, int) and u < 2):
                        act.wait_ge(pv_ready, (u - 1) * NG)
                    scale = rstd[:r, par, t:t + 1] if layer == 0 else 1.0 / WS
                    act.activation(vbuf[:r, par, t, :, 0:DK], p_proj[:r, a % 2, :].rearrange("p (h d) -> p h d", d=DK),
                                   ACT.Identity, scale=scale).then_inc(v_hi_made, 1)

            def out_hi(s):
                act.wait_ge(o_made, (s - 1) * NG)
                if not (isinstance(s, int) and s == 2):
                    act.wait_ge(misc_ready, sl.misc_count(s - 1, ("out", 0)))
                act.copy(oparts[:SQ, 0, :], o32[:SQ, :]).then_inc(o_hi_made, 1)

            def step(s, par, kind):
                prep, proj, has_scores, outs = kind
                for j in range(sl.n):
                    g, t = divmod(j, KT)
                    if has_scores:
                        exp(s - 1, g, t)
                        if j > 0:
                            prob_hi(s - 1, *divmod(j - 1, KT))
                    if prep and j + 2 in sl.ctx:
                        ctx_hi(s + 1, sl.ctx[j + 2])
                    if prep and j in sl.bc:
                        rstd_row(s, par, sl.bc[j])
                    if outs and j == sl.out_t - 2:
                        out_hi(s)
                    if proj:
                        for a in sl.evac[j]:
                            evacuate(s, par, a)
                if has_scores:
                    prob_hi(s - 1, NG - 1, KT - 1)

            act.wait_ge(padded, 1)
            if layer == 0:
                for t in range(KT):
                    ctx_hi(0, t)
                for n in range(2):
                    rstd_row(-1, 1, n)
            steps(act, step)

        @blk.vector
        def _(dve):
            def ctx_stats(b, t):
                r = KROWS[t]
                if t == 0 and not (isinstance(b, int) and b == 0):
                    dve.wait_ge(var_made, b)
                dve.wait_ge(c_loaded[t % 3], 32 * b + 16 * (t // 3 + 1))
                dve.bn_stats(stats[:r, t % 3, :], c32[:r, t % 3, :]).then_inc(stats_made, 1)
                dve.drain()
                dve.bn_aggr(mv[:r, t, :], stats[:r, t % 3, :]).then_inc(mv_made, 1)

            def ctx_var(b):
                dve.wait_ge(mv_made, (b + 1) * KT)
                if not (isinstance(b, int) and b == 0):
                    dve.wait_ge(rstd_made, b)
                dve.tensor_scalar(var[:], mv[:, :, 1], eps, WS * WS, ALU.add, ALU.mult).then_inc(var_made, 1)

            def rstd_diag(b, par):
                dve.wait_ge(rstd_made, b + 1)
                if not (isinstance(b, int) and b == 0):
                    dve.wait_ge(misc_ready, sl.misc_count(b - 2, ("bc", 1)))
                for t in range(KT):
                    r = KROWS[t]
                    dve.tensor_scalar(rdiag[:r, t, :], ident[:r, :], rstd[:r, par, t:t + 1], None, ALU.mult).then_inc(rdiag_made, 1)

            def ctx_copy(s, par, t):
                r = KROWS[t]
                dve.wait_ge(misc_ready, sl.misc_count(s, ("ctx", t)))
                if t == 0 and not (isinstance(s, int) and s < 1):
                    dve.wait_ge(proj_ready, NPROJ * s)
                    dve.wait_ge(ctxT_moved[1 - par], 16 * ((s + 1) // 2) if isinstance(s, int) else 8 * (s - par) + 16 * par)
                dve.tensor_copy(ctxT[:, 1 - par, :, :, P * t:P * t + r],
                                misc16.rearrange("p (a k s) -> p a k s", a=2, k=ET)[:, :, :, :r]).then_inc(misc_freed, 1)

            def take_max(u, g, hh):
                n_use = (u * NG + g) * HG + hh
                dve.wait_ge(max_ready, n_use + 1)
                if hh == 0 and not (isinstance(u, int) and n_use == 0):
                    dve.wait_ge(nm_made, u * NG + g)
                dve.tensor_reduce(nmax[:SQ, hh:hh + 1], p_max[:SQ, :, :HALF], AX.XY, ALU.max, negate=True).then_inc(max_made, 1)

            def split_max(s, u, g, prev):
                G = u * NG + g
                dve.wait_ge(max_made, (G + 1) * HG)
                if prev is not None:
                    dve.wait_ge(misc_ready, prev)
                dve.tensor_scalar(nmax_parts[:SQ, MR:MR + HG], nmax[:SQ, :], -score_bias, None, ALU.add).then_inc(nm_hi_made, 1)
                dve.wait_ge(nm_hi_made, G + 1)
                dve.scalar_tensor_tensor(nmax_parts[:SQ, MR + HG:MR + 2 * HG], nmax[:SQ, :], -score_bias,
                                         nmax_parts[:SQ, MR:MR + HG], ALU.add, ALU.subtract).then_inc(nm_made, 1)

            def place_max(s, use, par, g):
                dve.wait_ge(misc_ready, sl.misc_count(s, use))
                src = misc16[MR:MR + 2 * HG, :SQ].rearrange("p (o q) -> p o q", o=1).to_broadcast([2 * HG, HG, SQ])
                dve.tensor_copy(qstack[-1][MR:MR + 2 * HG, par, HG * g:HG * g + HG, :], src).then_inc(misc_freed, 1)

            def k_lo(u, m):
                dve.wait_ge(k_hi_made, 4 * u + (m + 1))
                dve.scalar_tensor_tensor(knat[:, m % 2, 1, :], kscaled[:, m % 2, :], kb_col[:, m:m + 1],
                                         knat[:, m % 2, 0, :], ALU.add, ALU.subtract).then_inc(k_lo_made, 1)

            def evacuate(u, par, a):
                if a < 8:
                    m, n = divmod(a, 2)
                    cols = slice(n * HALF, (n + 1) * HALF)
                    if layer == 0:
                        dve.wait_ge(proj_ready, NPROJ * u + (a + 1))
                        if n == 0:
                            if a == 0:
                                dve.wait_ge(misc_freed, sl.misc_count(u - 1, ("bc", 1)))
                            if not (isinstance(u, int) and 4 * u + m < 2):
                                dve.wait_ge(k_hi_made, 4 * u + (m - 1))
                                dve.wait_ge(k_lo_made, 4 * u + (m - 1))
                        dve.tensor_tensor(kscaled[:, m % 2, cols], p_proj[:, a % 2, :HALF], rrow[:, par, cols],
                                          ALU.mult).then_inc(proj_freed, 1)
                    else:
                        dve.wait_ge(k_hi_made, 8 * u + (a + 1))
                        ins = dve.scalar_tensor_tensor(knat[:, m % 2, 1, cols], p_proj[:, a % 2, :HALF], 1.0 / WS,
                                                       knat[:, m % 2, 0, cols], ALU.mult, ALU.subtract)
                        ins.then_inc(proj_freed, 1)
                else:
                    t = a - 8
                    r = KROWS[t]
                    dve.wait_ge(v_hi_made, KT * u + (t + 1))
                    scale = rstd[:r, par, t:t + 1] if layer == 0 else 1.0 / WS
                    dve.scalar_tensor_tensor(vbuf[:r, par, t, :, DK + 1:], p_proj[:r, a % 2, :].rearrange("p (h d) -> p h d", d=DK),
                                             scale, vbuf[:r, par, t, :, 0:DK], ALU.mult, ALU.subtract).then_inc(proj_freed, 1)

            def copy_pv(u, g):
                G = u * NG + g
                dve.wait_ge(pv_ready, G + 1)
                if not (isinstance(u, int) and G < 2):
                    dve.wait_ge(o_normed if layer == 0 else o_made, G - 1)
                dve.tensor_copy(pv_sb[:SQ, g % 2, :, :], p_pv[:SQ, :HG * OC].rearrange("p (h c) -> p h c", c=OC)).then_inc(pv_copied, 1)
                dve.wait_ge(pv_copied, G + 1)
                dve.reciprocal(orecip[:SQ, g % 2, :], pv_sb[:SQ, g % 2, :, DK]).then_inc(recip_made, 1)

            def out_copy(s, par, b):
                dve.wait_ge(misc_ready, sl.misc_count(s, ("out", 0)))
                src = misc16.rearrange("p (a k s) -> p a k s", a=2, k=ET)[:, :, :, :SQ]
                k0 = 0 if layer == 0 else ET * par
                dve.tensor_copy(outT[:, :, k0:k0 + ET, bass.ds(b * SQ, SQ)], src).then_inc(misc_freed, 1)

            def step(s, par, kind, batch=None):
                prep, proj, has_scores, outs = kind
                for j in range(sl.n):
                    g, t = divmod(j, KT)
                    if prep and j in sl.ctx:
                        ctx_copy(s, par, sl.ctx[j])
                    if prep and j + 2 in sl.ctx:
                        ctx_stats(s + 1, sl.ctx[j + 2])
                    if prep and j == sl.var_t:
                        ctx_var(s + 1)
                    if prep and j == sl.diag_t:
                        rstd_diag(s + 1, 1 - par)
                    if outs and j == sl.out_t:
                        out_copy(s, par, s - 2 if layer == 0 else batch)
                    if has_scores and j > 0 and (t - 1) % 2:
                        prob_lo(dve, s - 1, *divmod(j - 1, KT))
                    if t == MAX_T:
                        if g < NG - 1 and has_scores:
                            place_max(s, ("max", g), 1 - par, g + 1)
                        if g == NG - 1 and proj:
                            place_max(s, ("max", g), par, 0)
                    if g < NG - 1:
                        nxt = (s - 1, g + 1) if has_scores else None
                    else:
                        nxt = (s, 0) if proj else None
                    if nxt and t < HG:
                        take_max(*nxt, t)
                        if t == HG - 1:
                            if g > 0:
                                prev = sl.misc_count(s, ("max", g - 1)) if has_scores else None
                            else:
                                prev = sl.misc_count(s - 1, ("max", NG - 1))
                            split_max(s, *nxt, prev)
                    if t == PV_T + HG - 1:
                        if g == 0 and outs:
                            copy_pv(s - 2, NG - 1)
                        if g > 0 and has_scores:
                            copy_pv(s - 1, g - 1)
                    if proj:
                        if layer == 0 and j in sl.k_lo:
                            k_lo(s, sl.k_lo[j])
                        for a in sl.evac[j]:
                            evacuate(s, par, a)
                if has_scores:
                    prob_lo(dve, s - 1, NG - 1, KT - 1)

            dve.tensor_tensor(onehot[MR:MR + 2 * HG, :], ident[MR:MR + 2 * HG, MR:MR + HG],
                              ident[MR:MR + 2 * HG, MR + HG:MR + 2 * HG], ALU.add).then_inc(onehot_made, 1)
            dve.memset(probs[:, :, :, :, HG * SQ:], 0.0)
            dve.memset(nmax_parts[:], 0.0)
            if layer == 0:
                dve.memset(mv[:], 1.0)
                dve.memset(half_power[:], -0.5)
            dve.memset(vbuf[:, :, :, :, DK:DK + 1], 1.0)
            dve.memset(bias_col[:], score_bias).then_inc(padded, 1)
            dve.wait_ge(onehot_made, 1)
            for hh in range(HG):
                dve.tensor_copy(kstack[-1][MR:MR + 2 * HG, 0, hh, :],
                                onehot[MR:MR + 2 * HG, hh:hh + 1].to_broadcast([2 * HG, SK])).then_inc(onehot_seeded, 1)
            dve.wait_ge(padded, 1)
            if layer == 0:
                for t in range(KT):
                    ctx_stats(0, t)
                    if t >= 1:
                        ctx_copy(-1, 1, t - 1)
                ctx_var(0)
                rstd_diag(0, 0)
                ctx_copy(-1, 1, KT - 1)
                steps(dve, step)
            else:
                for s in range(2):
                    step(s, s, sl.kind(s))
                with dve.Fori(1, U // 2) as i:
                    for par in range(2):
                        step(2 * i + par, par, sl.kind(2), i - 1)
                for s in range(U, U + 2):
                    step(s, s % 2, sl.kind(s), s // 2 - 1)

        @blk.gpsimd
        def _(pool):
            def ctx_lo(b, t):
                r = KROWS[t]
                pool.wait_ge(c_hi_made, b * KT + (t + 1))
                pool.tensor_tensor(cparts[:r, t % 2, 1, :], c32[:r, t % 3, :], cparts[:r, t % 2, 0, :], ALU.subtract).then_inc(c_lo_made, 1)

            def ctx_rstd(b, par):
                pool.wait_ge(var_made, b + 1)
                if not (isinstance(b, int) and b < 2):
                    pool.wait_ge(proj_freed, NPROJ * (b - 1))
                pool.tensor_tensor(rstd[:, par, :], var[:], half_power[:], ALU.pow).then_inc(rstd_made, 1)

            def normalise(u, g):
                G = u * NG + g
                cols = slice(g * HG * DK, (g + 1) * HG * DK)
                out = o32[:SQ, cols].rearrange("p (h d) -> p h d", d=DK)
                recip = orecip[:SQ, g % 2, :].rearrange("p (h o) -> p h o", o=1).to_broadcast([SQ, HG, DK])
                pool.wait_ge(recip_made, G + 1)
                if g == 0 and not (isinstance(u, int) and u == 0):
                    pool.wait_ge(o_lo_made, u)
                if layer == 0:
                    pool.tensor_tensor(osum[:SQ], pv_sb[:SQ, g % 2, :, :DK], pv_sb[:SQ, g % 2, :, DK + 1:], ALU.add).then_inc(o_summed, 1)
                    pool.wait_ge(o_summed, G + 1)
                    pool.tensor_tensor(osum[:SQ], osum[:SQ], recip, ALU.mult).then_inc(o_normed, 1)
                    pool.wait_ge(o_normed, G + 1)
                    pool.tensor_tensor(o32[:SQ, cols], osum[:SQ].rearrange("p h d -> p (h d)"), vb_row[:SQ, cols], ALU.add).then_inc(o_made, 1)
                    pool.wait_ge(o_made, G + 1)
                else:
                    pool.tensor_tensor(out, pv_sb[:SQ, g % 2, :, :DK], recip, ALU.mult).then_inc(o_made, 1)

            def out_lo(s):
                pool.wait_ge(o_hi_made, s - 1)
                pool.tensor_tensor(oparts[:SQ, 1, :], o32[:SQ, :], oparts[:SQ, 0, :], ALU.subtract).then_inc(o_lo_made, 1)

            def step(s, par, kind):
                prep, proj, has_scores, outs = kind
                for j in range(sl.n):
                    g, t = divmod(j, KT)
                    if has_scores and j > 0 and (t - 1) % 2 == 0:
                        prob_lo(pool, s - 1, *divmod(j - 1, KT))
                    if prep and j + 2 in sl.ctx:
                        ctx_lo(s + 1, sl.ctx[j + 2])
                    if prep and j == sl.var_t:
                        ctx_rstd(s + 1, 1 - par)
                    if t == PV_T + HG - 1:
                        if g == 0 and outs:
                            normalise(s - 2, NG - 1)
                        if g > 0 and has_scores:
                            normalise(s - 1, g - 1)
                    if outs and j == sl.out_t - 1:
                        out_lo(s)

            if layer == 0:
                for t in range(KT):
                    ctx_lo(0, t)
                ctx_rstd(0, 0)
            steps(pool, step)


def bass_two_cross_attentions(nc, x, ctx, wq, bq, wk, bk, wv, bv, wo, bo, ln1_g, ln1_b, ln2_g, ln2_b, w1, b1, w2, b2,
                              wq1, wk1, wv1, wfc, gamma, beta, out):
    rows = lambda a: a.rearrange("b s e -> (b s) e")
    by_tile = lambda w: w.rearrange("(k p) n -> p k n", p=P)
    x_rows, out_rows = rows(x), rows(out)
    q0_d = nc.dram_tensor("q0_parts", [2, P, ET, ROWS], F16, kind="Internal").ap()
    q1_d = nc.dram_tensor("q1_parts", [2, P, 2 * ET, ROWS], F16, kind="Internal").ap()
    ctxT_d = nc.dram_tensor("ctxT_parts", [B, P, 2 * ET * SK], F16, kind="Internal").ap()
    x2_d = nc.dram_tensor("layer0_out", [ROWS, E], F32, kind="Internal").ap()

    def columns(w):
        v = by_tile(w)
        return [v[:, :, c:c + E] for c in range(0, w.shape[1], E)]

    def part_jobs(pieces, parts):
        return [(piece, parts[:, 0, :, c * E:(c + 1) * E], parts[:, 1, :, c * E:(c + 1) * E]) for c, piece in enumerate(pieces)]

    with Scope(nc, "kernel") as top:
        ident = top.sb("ident", [P, P])
        ident16 = top.sb("ident16", [P, P], F16)
        ones_mean = top.sb("ones_mean", [P, P])
        ones32 = top.sb("ones32", [P, P])
        make_constants(nc, ident, ident16, ones_mean, ones32)

        def load_vectors(name, jobs):
            with Scope(nc, name) as sc:
                loaded = sc.sem("loaded")
                blk = sc.block()

                @blk.sync
                def _(sp):
                    for dst, src in jobs:
                        if dst.shape[1] == src.shape[0]:
                            sp.dma_start(dst[:], src.partition_broadcast(P)).then_inc(loaded, 16)
                        else:
                            sp.dma_start(dst[:], src.rearrange("(k p) -> p k", p=P),
                                         allow_slow_non_contiguous=True).then_inc(loaded, 16)
                    sp.wait_ge(loaded, 16 * len(jobs))

        with Scope(nc, "attn_out0") as keep0:
            o0T = keep0.sb("o0T", [P, 2, ET, ROWS], F16)
            with Scope(nc, "l0") as l0:
                w_k = l0.sb("w_k", [P, 2, ET, E], F16)
                w_v = l0.sb("w_v", [P, 2, ET, E], F16)
                kb_col = l0.sb("kb_col", [P, ET])
                vb_row = l0.sb("vb_row", [P, E])
                with Scope(nc, "q0") as q0:
                    w_q = q0.sb("w_q", [P, 2, ET, E], F16)
                    g_row, b_row = q0.sb("g_row", [P, E]), q0.sb("b_row", [P, E])
                    bv_row = q0.sb("bv_row", [P, E])
                    g_col, b_col, bk_col, bq_col = (q0.sb(n, [P, ET]) for n in ("g_col", "b_col", "bk_col", "bq_col"))
                    bqs_col = q0.sb("bqs_col", [P, ET])
                    xT = q0.sb("xT", [P, 2, ET, ROWS], F16)
                    qT = q0.sb("qT", [P, 2, ET, ROWS], F16)
                    load_vectors("vec0", [(g_row, ln1_g), (b_row, ln1_b), (bv_row, bv), (g_col, ln1_g), (b_col, ln1_b),
                                          (bk_col, bk), (bq_col, bq)])
                    scale0 = 32.0 ** -0.5
                    scale_column(nc, bqs_col, bq_col, scale0)
                    fold_norm_weights(nc, wk, wv, g_col, b_col, bk_col, bv_row, ones_mean, w_k, w_v, kb_col, vb_row)
                    split_weights(nc, "split_q0", part_jobs(columns(wq), w_q))
                    rows_stage(nc, "rows_q0", ident16, x_rows, norm=(1e-5, g_row, b_row), xT=xT)
                    columns_stage(nc, "cols_q0", xT, w_q, ET, ACT.Identity, bqs_col, scale0 / WS, qT, store=q0_d)
                attention(nc, 0, ctx, ctxT_d, q0_d, w_k, w_v, kb_col, vb_row, ident, ident16, ones32, 1e-5, 0.0, o0T)
            with Scope(nc, "mlp") as m:
                hT = m.sb("hT", [P, 2, FT, ROWS], F16)
                x1 = m.sb("x1", [P, RT, E])
                b2_row = m.sb("b2_row", [P, E])
                b1_col = m.sb("b1_col", [P, FT])
                with Scope(nc, "mlp_in") as mi:
                    yT = mi.sb("yT", [P, 2, ET, ROWS], F16)
                    w1p = mi.sb("w1", [P, 2, ET, FF], F16)
                    with Scope(nc, "proj0") as pr:
                        w_o = pr.sb("w_o", [P, 2, ET, E], F16)
                        g_row, b_row, bo_row = (pr.sb(n, [P, E]) for n in ("g_row", "b_row", "bo_row"))
                        load_vectors("vec1", [(g_row, ln2_g), (b_row, ln2_b), (bo_row, bo), (b2_row, b2), (b1_col, b1)])
                        split_weights(nc, "split_wo", part_jobs(columns(wo), w_o))
                        rows_stage(nc, "rows_wo", ident16, x_rows, w=w_o, lhs=o0T, bias=bo_row, norm=(1e-5, g_row, b_row),
                                   keep=x1, xT=yT)
                    split_weights(nc, "split_w1", part_jobs(columns(w1), w1p))
                    columns_stage(nc, "cols_w1", yT, w1p, FT, ACT.Gelu, b1_col, 1.0 / WS, hT)
                with Scope(nc, "mlp_out") as mo:
                    w2p = mo.sb("w2", [P, 2, FT, E], F16)
                    xT = mo.sb("xT", [P, 2, ET, ROWS], F16)
                    w2_tiles = by_tile(w2)
                    split_weights(nc, "split_w2", [(w2_tiles[:, k:k + ET, :], w2p[:, 0, k:k + ET, :], w2p[:, 1, k:k + ET, :])
                                                   for k in range(0, FT, ET)])
                    rows_stage(nc, "rows_w2", ident16, None, w=w2p, lhs=hT, res=x1, bias=b2_row, store=x2_d, xT=xT)
                    with Scope(nc, "q1") as q1:
                        w_q = q1.sb("w_q", [P, 2, ET, 2 * E], F16)
                        qT = q1.sb("qT", [P, 2, 2 * ET, ROWS], F16)
                        split_weights(nc, "split_q1", part_jobs(columns(wq1), w_q))
                        columns_stage(nc, "cols_q1", xT, w_q, 2 * ET, ACT.Identity, None, 64.0 ** -0.5 / WS, qT, store=q1_d)
        with Scope(nc, "attn_out1") as keep1:
            o1T = keep1.sb("o1T", [P, 2, 2 * ET, ROWS], F16)
            with Scope(nc, "l1") as l1:
                w_k = l1.sb("w_k", [P, 2, ET, 2 * E], F16)
                w_v = l1.sb("w_v", [P, 2, ET, 2 * E], F16)
                split_weights(nc, "split_kv1", part_jobs(columns(wk1), w_k) + part_jobs(columns(wv1), w_v))
                score_bias = -0.5 * 2.0 ** 2 / (0.5 * 4.0) ** 2
                attention(nc, 1, ctx, ctxT_d, q1_d, w_k, w_v, None, None, ident, ident16, ones32, None, score_bias, o1T)
            with Scope(nc, "l1_out") as lo:
                w_fc = lo.sb("w_fc", [P, 2, 2 * ET, E], F16)
                g_row, b_row = lo.sb("g_row", [P, E]), lo.sb("b_row", [P, E])
                load_vectors("vec2", [(g_row, gamma), (b_row, beta)])
                fc_tiles = by_tile(wfc)
                split_weights(nc, "split_fc", [(fc_tiles[:, k:k + ET, :], w_fc[:, 0, k:k + ET, :], w_fc[:, 1, k:k + ET, :])
                                               for k in range(0, 2 * ET, ET)])
                rows_stage(nc, "rows_fc", ident16, x2_d, w=w_fc, lhs=o1T, norm=(1e-6, g_row, b_row), store=out_rows)


def scale_column(nc, dst, src, factor):
    with Scope(nc, "scale_bias") as sc:
        blk = sc.block()

        @blk.vector
        def _(dve):
            dve.tensor_scalar(dst[:], src[:], factor, None, ALU.mult)


_INS = ["x", "ctx_1024", "L0_xattn_wq", "L0_xattn_bq", "L0_xattn_wk", "L0_xattn_bk", "L0_xattn_wv", "L0_xattn_bv",
        "L0_xattn_wo", "L0_xattn_bo", "L0_xattn_ln1_g", "L0_xattn_ln1_b", "L0_xattn_ln2_g", "L0_xattn_ln2_b",
        "L0_xattn_w1", "L0_xattn_b1", "L0_xattn_w2", "L0_xattn_b2", "L1_xattn_Wq", "L1_xattn_Wk", "L1_xattn_Wv",
        "L1_xattn_Wfc", "L1_xattn_gamma", "L1_xattn_beta"]


def kernel(**inputs):
    import numpy as _np
    import concourse.bacc as _bacc
    from concourse import mybir as _mybir
    from concourse.bass_utils import run_bass_kernel_spmd as _run

    nc = _bacc.Bacc("TRN2", target_bir_lowering=False, num_devices=1)
    arrays, args = {}, []
    for name in _INS:
        a = _np.ascontiguousarray(inputs[name])
        arrays[f"in_{name}_dram"] = a
        args.append(nc.dram_tensor(f"in_{name}_dram", a.shape, _mybir.dt.from_np(a.dtype), kind="ExternalInput").ap())
    args.append(nc.dram_tensor("out_0_dram", (B, SQ, E), F32, kind="ExternalOutput").ap())
    bass_two_cross_attentions(nc, *args)
    r = _run(nc, [arrays], core_ids=[0])
    return r.results[0]["out_0_dram"]
```

```python
from contextlib import ExitStack

import concourse.bass as bass
from concourse import mybir

P = 128
B, SQ, SK, E = 8, 100, 722, 512
ROWS = B * SQ
ET = E // P
KT = -(-SK // P)
KROWS = [min(P, SK - P * t) for t in range(KT)]
HALF = SK // 2
RT = -(-ROWS // P)
RROWS = [min(P, ROWS - P * t) for t in range(RT)]
QHALF = ROWS // 2
H = 16
FF = 4 * E
FT = FF // P
WS = 256.0
HG = 4
MAX_T, PV_T = 4, 2

F32, F16 = mybir.dt.float32, mybir.dt.float16
ALU = mybir.AluOpType
ACT = mybir.ActivationFunctionType
AX = mybir.AxisListType
PARTS = ((0, 0), (0, 1), (1, 0))


class Scope:

    def __init__(self, nc, name):
        self.nc, self.name, self.stack, self.sems = nc, name, ExitStack(), []

    def __enter__(self):
        return self

    def __exit__(self, *a):
        self.stack.close()
        if self.sems:
            self.nc.clear_and_free_semaphores(self.sems)
            self.nc.all_engine_barrier()

    def sb(self, name, shape, dt=F32):
        return self.stack.enter_context(self.nc.sbuf_tensor(f"{self.name}_{name}", shape, dt))

    def ps(self, name, shape, dt=F32):
        return self.stack.enter_context(self.nc.psum_tensor(f"{self.name}_{name}", shape, dt))

    def sem(self, name):
        self.sems.append(self.nc.alloc_semaphore(f"{self.name}_{name}"))
        return self.sems[-1]

    def block(self):
        return self.stack.enter_context(self.nc.Block())


def make_constants(nc, ident, ident16, ones_mean, ones32):
    with Scope(nc, "const") as sc:
        zeroed, ident_made = sc.sem("zeroed"), sc.sem("ident_made")
        blk = sc.block()

        @blk.gpsimd
        def _(pool):
            pool.memset(ident[:], 0.0).then_inc(zeroed, 1)
            pool.wait_ge(zeroed, 1)
            pool.affine_select(out=ident[:], in_=ident[:], compare_op=ALU.not_equal, fill=1.0, base=0,
                               pattern=[[-1, P]], channel_multiplier=1).then_inc(ident_made, 1)

        @blk.vector
        def _(dve):
            dve.memset(ones_mean[:], 1.0 / E)
            dve.memset(ones32[:], 1.0)
            dve.wait_ge(ident_made, 1)
            dve.tensor_copy(ident16[:], ident[:])


class WeightSplit:

    def __init__(self, sc, jobs):
        self.jobs = list(jobs)
        if self.jobs:
            self.w32 = sc.sb("w32", [P, 2, ET, E])
            self.loaded = [sc.sem(f"w_loaded{i}") for i in range(2)]
            self.hi_made, self.lo_made = sc.sem("w_hi_made"), sc.sem("w_lo_made")

    def load(self, sp, n):
        if 0 <= n < len(self.jobs):
            if n >= 2:
                sp.wait_ge(self.lo_made, n - 1)
            sp.dma_start(self.w32[:, n % 2, :self.jobs[n][0].shape[1]], self.jobs[n][0]).then_inc(self.loaded[n % 2], 16)

    def hi(self, act, n):
        if 0 <= n < len(self.jobs):
            act.wait_ge(self.loaded[n % 2], 16 * (n // 2 + 1))
            act.activation(self.jobs[n][1], self.w32[:, n % 2, :self.jobs[n][1].shape[1]], ACT.Identity, scale=WS).then_inc(self.hi_made, 1)

    def lo(self, dve, n):
        if 0 <= n < len(self.jobs):
            _src, hi, lo = self.jobs[n]
            dve.wait_ge(self.hi_made, n + 1)
            dve.scalar_tensor_tensor(lo, self.w32[:, n % 2, :lo.shape[1]], WS, hi, ALU.mult, ALU.subtract).then_inc(self.lo_made, 1)


class NormFold:

    def __init__(self, sc, sources, g_col, b_col, bk_col, bv_row, bq_col, bqs_col, q_scale, ones_mean, weights, kb_col, vb_row):
        self.sources, self.weights, self.ones_mean, self.q_scale = sources, weights, ones_mean, q_scale
        self.g_col, self.b_col, self.bk_col, self.bv_row, self.bq_col, self.bqs_col = g_col, b_col, bk_col, bv_row, bq_col, bqs_col
        self.kb_col, self.vb_row = kb_col, vb_row
        self.w32 = sc.sb("fold_w32", [P, 2, ET, E])
        self.wg = sc.sb("fold_wg", [P, 2, ET, E])
        self.b_wide = sc.sb("b_wide", [P, ET, P])
        self.pbias = sc.ps("pbias", [P, 2, 512])
        self.pmean = sc.ps("pmean", [P, 2, 512])
        self.loaded = [sc.sem(f"fold_loaded{i}") for i in range(2)]
        self.b_widened, self.scaled, self.bias_ready, self.mean_ready, self.centred, self.hi_made = (
            sc.sem(n) for n in ("b_widened", "w_scaled", "bias_ready", "mean_ready", "w_centred", "fold_hi_made"))

    def load(self, sp):
        for n, src in enumerate(self.sources):
            sp.dma_start(self.w32[:, n], src).then_inc(self.loaded[n], 16)

    def vector(self, dve, part):
        if part == 0:
            dve.tensor_scalar(self.bqs_col[:], self.bq_col[:], self.q_scale, None, ALU.mult)
            for k in range(ET):
                dve.tensor_copy(self.b_wide[:, k, :], self.b_col[:, k:k + 1].to_broadcast([P, P])).then_inc(self.b_widened, 1)
        if part in (1, 2):
            n = part - 1
            dve.wait_ge(self.loaded[n], 16)
            for k in range(ET):
                dve.tensor_scalar(self.wg[:, n, k, :], self.w32[:, n, k, :], self.g_col[:, k:k + 1], None, ALU.mult).then_inc(self.scaled, 1)
        if part in (3, 4):
            n = part - 3
            dve.wait_ge(self.bias_ready, n + 1)
            if n == 0:
                dve.tensor_tensor(self.kb_col[:], self.pbias[:, 0, 0:ET], self.bk_col[:], ALU.add)
            else:
                dve.tensor_tensor(self.vb_row[:], self.pbias[:, 1, :], self.bv_row[:], ALU.add)
            dve.wait_ge(self.mean_ready, n + 1)
            for k in range(ET):
                dve.tensor_tensor(self.w32[:, n, k, :], self.wg[:, n, k, :], self.pmean[:, n, :], ALU.subtract).then_inc(self.centred, 1)
        if part in (5, 6):
            n = part - 5
            w = self.weights[n]
            dve.wait_ge(self.hi_made, n + 1)
            dve.scalar_tensor_tensor(w[:, 1], self.w32[:, n], WS, w[:, 0], ALU.mult, ALU.subtract)

    def tensor(self, pe, n):
        if n not in (0, 1):
            return
        pe.wait_ge(self.b_widened, ET)
        pe.wait_ge(self.loaded[n], 16)
        if n == 0:
            for m in range(ET):
                for k in range(ET):
                    last = pe.matmul(self.pbias[:, 0, m:m + 1], self.w32[:, 0, k, m * P:(m + 1) * P], self.b_col[:, k:k + 1],
                                     start=(k == 0), stop=(k == ET - 1))
        else:
            for k in range(ET):
                last = pe.matmul(self.pbias[:, 1, :], self.b_wide[:, k, :], self.w32[:, 1, k, :], start=(k == 0), stop=(k == ET - 1))
        last.then_inc(self.bias_ready, 1)
        pe.wait_ge(self.scaled, ET * (n + 1))
        for k in range(ET):
            last = pe.matmul(self.pmean[:, n, :], self.ones_mean[:], self.wg[:, n, k, :], start=(k == 0), stop=(k == ET - 1))
        last.then_inc(self.mean_ready, 1)

    def scalar(self, act, n):
        if n in (0, 1):
            act.wait_ge(self.centred, ET * (n + 1))
            act.activation(self.weights[n][:, 0], self.w32[:, n], ACT.Identity, scale=WS).then_inc(self.hi_made, 1)


def rows_stage(nc, name, ident16, res_d, w=None, lhs=(), res=None, bias=None, norm=None, keep=None, store=None, xT=None,
               vectors=(), late_vectors=(), split=(), fold=None):
    lhs_tiles = [(part, k) for part in lhs for k in range(part.shape[2])]
    kt = len(lhs_tiles)
    with Scope(nc, name) as sc:
        if res is None:
            res = sc.sb("res", [P, RT, E])
        y = keep if keep is not None else (sc.sb("y", [P, RT, E]) if w is not None else res)
        z = sc.sb("z", [P, RT, E]) if norm else y
        hi = sc.sb("hi", [P, 3, E], F16)
        lo = sc.sb("lo", [P, 3, E], F16)
        stats = sc.sb("stats", [P, RT, 6])
        mv = sc.sb("mv", [P, RT, 2])
        rstd = sc.sb("rstd", [P, RT])
        half_power = sc.sb("half_power", [P, 1])
        weight_split = WeightSplit(sc, split)
        folding = NormFold(sc, *fold) if fold else None
        late_total = 16 * len(late_vectors)
        acc = sc.ps("acc", [P, 4, 512]) if w is not None else None
        tr = [sc.ps(f"tr{i}", [P, 2, ET, P], F16) for i in range(2)]
        loaded = [sc.sem(f"loaded{t}") for t in range(RT)]
        late_loaded = sc.sem("late_loaded")
        names = ("vectors_loaded", "power_set", "var_made", "acc_ready", "summed", "biased", "stats_made", "mv_made",
                 "rstd_made", "centred", "scaled", "normed", "hi_made", "lo_made", "tr_ready", "tr_freed", "stored")
        (vectors_loaded, power_set, var_made, acc_ready, summed, biased, stats_made, mv_made, rstd_made, centred,
         scaled, normed, hi_made, lo_made, tr_ready, tr_freed, stored) = (sc.sem(n) for n in names)
        blk = sc.block()

        def wait_y(eng, T):
            if w is not None:
                eng.wait_ge(summed, T + 1)
            else:
                eng.wait_ge(loaded[T], 16)

        def wait_z(eng, T):
            if norm:
                eng.wait_ge(normed, T + 1)
            else:
                wait_y(eng, T)

        @blk.sync
        def _(sp):
            def load_vectors(jobs, sem):
                for dst, src in jobs:
                    if dst.shape[1] == src.shape[0]:
                        sp.dma_start(dst[:], src.partition_broadcast(P)).then_inc(sem, 16)
                    else:
                        sp.dma_start(dst[:], src.rearrange("(k p) -> p k", p=P), allow_slow_non_contiguous=True).then_inc(sem, 16)

            def load_res(T):
                r = RROWS[T]
                sp.dma_start(res[:r, T], res_d[P * T:P * T + r, :]).then_inc(loaded[T], 16)

            if res_d is not None:
                load_res(0)
            load_vectors(vectors, vectors_loaded)
            if res_d is not None:
                for T in range(1, RT):
                    load_res(T)
            load_vectors(late_vectors, late_loaded)
            if folding:
                folding.load(sp)
            for n in range(2):
                weight_split.load(sp, n)
            for T, r in enumerate(RROWS):
                weight_split.load(sp, 2 + T)
                if store is not None:
                    wait_z(sp, T)
                    sp.dma_start(store[P * T:P * T + r, :], z[:r, T]).then_inc(stored, 16)
            if store is not None:
                sp.wait_ge(stored, 16 * RT)
            if late_vectors:
                sp.wait_ge(late_loaded, late_total)

        @blk.tensor
        def _(pe):
            for i in range(RT + 2):
                if i < RT and w is not None:
                    r = RROWS[i]
                    if i >= 4:
                        pe.wait_ge(summed, i - 3)
                    n = 0
                    for k, (part, kk) in enumerate(lhs_tiles):
                        for a, b in PARTS:
                            last = pe.matmul(acc[:r, i % 4, :], part[:, a, kk, P * i:P * i + r], w[:, b, k, :],
                                             start=(n == 0), stop=(n == 3 * kt - 1))
                            n += 1
                    last.then_inc(acc_ready, 1)
                T = i - 2
                if T >= 0 and xT is not None:
                    r = RROWS[T]
                    pe.wait_ge(lo_made, T + 1)
                    if T >= 2:
                        pe.wait_ge(tr_freed, T - 1)
                    for a, part in enumerate((hi, lo)):
                        for k in range(ET):
                            last = pe.transpose(tr[T % 2][:, a, k, :r], part[:r, T % 3, k * P:(k + 1) * P], ident16[:r, :r])
                    last.then_inc(tr_ready, 1)
                if folding:
                    folding.tensor(pe, {2: 0, 4: 1}.get(i, 2))

        @blk.vector
        def _(dve):
            if norm:
                dve.wait_ge(vectors_loaded, 16 * len(vectors))
            for i in range(RT + 2):
                if i < RT:
                    T, r = i, RROWS[i]
                    if w is not None:
                        dve.wait_ge(acc_ready, T + 1)
                        if bias is not None:
                            dve.wait_ge(biased, T + 1)
                        elif res_d is not None:
                            dve.wait_ge(loaded[T], 16)
                        dve.scalar_tensor_tensor(y[:r, T], acc[:r, T % 4, :], 1.0 / WS, res[:r, T], ALU.mult,
                                                 ALU.add).then_inc(summed, 1)
                    if norm:
                        wait_y(dve, T)
                        dve.bn_stats(stats[:r, T, :], y[:r, T]).then_inc(stats_made, 1)
                        dve.wait_ge(stats_made, T + 1)
                        dve.bn_aggr(mv[:r, T, :], stats[:r, T, :]).then_inc(mv_made, 1)
                        dve.wait_ge(mv_made, T + 1)
                        dve.scalar_tensor_tensor(z[:r, T], y[:r, T], mv[:r, T, 0:1], norm[1][:r], ALU.subtract,
                                                 ALU.mult).then_inc(centred, 1)
                T = i - 1
                if 0 <= T < RT and xT is not None:
                    r = RROWS[T]
                    dve.wait_ge(hi_made, T + 1)
                    dve.tensor_tensor(lo[:r, T % 3], z[:r, T], hi[:r, T % 3], ALU.subtract).then_inc(lo_made, 1)
                T = i - 2
                if T >= 0 and xT is not None:
                    r = RROWS[T]
                    dve.wait_ge(tr_ready, T + 1)
                    dve.tensor_copy(xT[:, :, :, P * T:P * T + r], tr[T % 2][:, :, :, :r]).then_inc(tr_freed, 1)
                if folding and i == 1:
                    dve.wait_ge(late_loaded, late_total)
                if folding:
                    for part in ((), (0,), (1,), (2,), (), (3,), (), (4, 5), (6,))[i]:
                        folding.vector(dve, part)
                if not folding and i >= 1:
                    weight_split.lo(dve, i - 1)
            for n in range(0 if folding else RT + 1, len(weight_split.jobs)):
                weight_split.lo(dve, n)

        @blk.gpsimd
        def _(pool):
            pool.memset(half_power[:], -0.5).then_inc(power_set, 1)
            pool.wait_ge(power_set, 1)
            if vectors:
                pool.wait_ge(vectors_loaded, 16 * len(vectors))
            for i in range(-2, RT):
                T = i + 2
                if T < RT and bias is not None:
                    r = RROWS[T]
                    if res_d is not None:
                        pool.wait_ge(loaded[T], 16)
                    pool.tensor_tensor(res[:r, T], res[:r, T], bias[:r], ALU.add).then_inc(biased, 1)
                T = i
                if T >= 0 and norm:
                    eps, _g_row, b_row = norm
                    r = RROWS[T]
                    pool.wait_ge(mv_made, T + 1)
                    pool.tensor_scalar(rstd[:r, T:T + 1], mv[:r, T, 1:2], eps, None, ALU.add).then_inc(var_made, 1)
                    pool.wait_ge(var_made, T + 1)
                    pool.tensor_tensor(rstd[:r, T:T + 1], rstd[:r, T:T + 1], half_power[:r, :], ALU.pow).then_inc(rstd_made, 1)
                    pool.wait_ge(scaled, T + 1)
                    pool.tensor_tensor(z[:r, T], z[:r, T], b_row[:r], ALU.add).then_inc(normed, 1)

        @blk.scalar
        def _(act):
            for T, r in enumerate(RROWS):
                if norm:
                    act.wait_ge(rstd_made, T + 1)
                    act.wait_ge(centred, T + 1)
                    act.activation(z[:r, T], z[:r, T], ACT.Identity, scale=rstd[:r, T:T + 1]).then_inc(scaled, 1)
                if xT is not None:
                    wait_z(act, T)
                    if T >= 3:
                        act.wait_ge(tr_ready, T - 2)
                    act.copy(hi[:r, T % 3], z[:r, T]).then_inc(hi_made, 1)
                if folding:
                    folding.scalar(act, T - 5)
                else:
                    weight_split.hi(act, T)
            for n in range(0 if folding else RT, len(weight_split.jobs)):
                weight_split.hi(act, n)


def columns_stage(nc, name, xT, w, m_tiles, func, bias_col, scale, outT, store=None, split=()):
    kt = xT.shape[2]
    with Scope(nc, name) as sc:
        out32 = sc.sb("out32", [P, 3, QHALF])
        weight_split = WeightSplit(sc, split)
        acc = sc.ps("acc", [P, 4, 512])
        acc_ready, made, hi_made, lo_made, stored = (sc.sem(n) for n in ("acc_ready", "made", "hi_made", "lo_made", "stored"))
        blk = sc.block()
        uses = [(m, n) for m in range(m_tiles) for n in range(2)]
        side = {3 + 3 * n: n for n in range(len(weight_split.jobs))}

        @blk.tensor
        def _(pe):
            for u, (m, n) in enumerate(uses):
                if u >= 4:
                    pe.wait_ge(made, u - 3)
                j = 0
                for k in range(kt):
                    for a, b in PARTS:
                        last = pe.matmul(acc[:, u % 4, :QHALF], w[:, a, k, m * P:(m + 1) * P],
                                         xT[:, b, k, n * QHALF:(n + 1) * QHALF], start=(j == 0), stop=(j == 3 * kt - 1))
                        j += 1
                last.then_inc(acc_ready, 1)

        @blk.scalar
        def _(act):
            for u, (m, n) in enumerate(uses):
                act.wait_ge(acc_ready, u + 1)
                if u >= 3:
                    act.wait_ge(lo_made, u - 2)
                bias = bias_col[:, m:m + 1] if bias_col is not None else 0.0
                act.activation(out32[:, u % 3, :], acc[:, u % 4, :QHALF], func, bias=bias, scale=scale).then_inc(made, 1)
                if u in side:
                    weight_split.hi(act, side[u])

        @blk.vector
        def _(dve):
            for u, (m, n) in enumerate(uses):
                cols = slice(n * QHALF, (n + 1) * QHALF)
                dve.wait_ge(made, u + 1)
                dve.tensor_copy(outT[:, 0, m, cols], out32[:, u % 3, :]).then_inc(hi_made, 1)
                dve.wait_ge(hi_made, u + 1)
                dve.tensor_tensor(outT[:, 1, m, cols], out32[:, u % 3, :], outT[:, 0, m, cols], ALU.subtract).then_inc(lo_made, 1)
                if u in side:
                    weight_split.lo(dve, side[u])

        @blk.sync
        def _(sp):
            for n in range(len(weight_split.jobs)):
                weight_split.load(sp, n)
            if store is not None:
                count = 0
                for m in range(m_tiles):
                    sp.wait_ge(lo_made, 2 * m + 2)
                    count += store_queries(sp, store, outT, m, stored)
                sp.wait_ge(stored, 16 * count)


def store_queries(sp, store, qT, m, stored):
    dk = store.shape[0] // 3
    hpt = P // dk
    for j in range(hpt):
        head, rows = hpt * m + j, slice(dk * j, dk * j + dk)
        sp.dma_start(store[0:2 * dk, head, :].rearrange("(o p) r -> p o r", o=2),
                     qT[rows, 0, m:m + 1, :].to_broadcast([dk, 2, ROWS])).then_inc(stored, 16)
        sp.dma_start(store[2 * dk:, head, :], qT[rows, 1, m, :]).then_inc(stored, 16)
    return 2 * hpt


class Slots:

    def __init__(self, layer):
        self.layer = layer
        self.groups = 4 if layer == 0 else 2
        self.n = KT * self.groups
        self.heads = HG * self.groups
        at = [0, 1, 3, 4, 6, 7, 9, 10, 12, 13, 15, 16, 18, 21] if layer == 0 else [0, 0, 1, 1, 2, 2, 3, 3, 4, 6, 7, 8, 10, 11]
        self.proj = [[a for a in range(14) if at[a] == j] for j in range(self.n)]
        self.evac = [(self.proj[j - 1][-1:] if j else []) + self.proj[j][:-1] for j in range(self.n)]
        self.evac[-1] = self.evac[-1] + self.proj[-1][-1:]
        self.k_lo = {j + 1: a // 2 for j in range(self.n) for a in self.evac[j] if a < 8 and a % 2}
        self.ctx = {2: 0, 6: 1, 12: 2, 14: 3, 17: 4, 20: 5} if layer == 0 else {}
        self.var_t, self.diag_t = 19, 20
        self.bc = {22: 0, 23: 1} if layer == 0 else {}
        self.out_t = 9
        self.units = B if layer == 0 else 2 * B

    def misc(self, prep, proj, scores, outs):
        uses = []
        for j in range(self.n):
            g, t = divmod(j, KT)
            if prep and j in self.ctx:
                uses.append(("ctx", self.ctx[j]))
            if prep and j in self.bc:
                uses.append(("bc", self.bc[j]))
            if outs and j == self.out_t:
                uses.append(("out", 0))
            if t == MAX_T and (scores if g < self.groups - 1 else proj):
                uses.append(("max", g))
        return uses

    def kind(self, s):
        return (self.layer == 0 and s + 1 < self.units, s < self.units, 1 <= s <= self.units, s >= 2)

    def misc_count(self, s, use):
        before = KT + 2 if self.layer == 0 else 0
        if isinstance(s, int):
            if s < 0:
                return ([("ctx", t) for t in range(KT)] + [("bc", 0), ("bc", 1)]).index(use) + 1
            for q in range(s):
                before += len(self.misc(*self.kind(q)))
            return before + self.misc(*self.kind(s)).index(use) + 1
        for q in range(2):
            before += len(self.misc(*self.kind(q)))
        steady = self.misc(*self.kind(2))
        return (s - 2) * len(steady) + (before + steady.index(use) + 1)


def attention(nc, layer, ctx_d, ctxT_d, q_d, w_k, w_v, kb_col, vb_row, ident, ident16, ones32, eps, score_bias, outT,
              next_weights, queries=None):
    sl = Slots(layer)
    NG, NH, U = sl.groups, sl.heads, sl.units
    DK = 32 if layer == 0 else 64
    HPT = P // DK
    MR = 96 if layer == 0 else 64
    VC = 2 * DK + 1
    OC = VC if layer == 0 else DK + 1
    NPROJ = 14
    NSTACK = 3 * HPT
    NQ = layer + 1
    NSLOT = sl.n
    PW = HG * SQ + (P - SQ)

    with Scope(nc, f"attn{layer}") as sc:
        ctxT = sc.sb("ctxT", [P, 2, 2, ET, SK], F16)
        knat = sc.sb("knat", [P, 4, 2, SK], F16)
        if layer == 0:
            kstack = [sc.sb("kstack", [P, 2, NH, SK], F16)]
            qstack = [sc.sb("qstack", [P, 2, NH, SQ], F16)]
        else:
            kstack = [sc.sb("kstack_a", [P, 2, NH, SK], F16), sc.sb("kstack_b", [P, 2, NH, SK], F16)]
            qstack = [sc.sb("qstack_a", [P, 2, NH, SQ], F16), sc.sb("qstack_b", [P, 2, NH, SQ], F16)]
        vbuf = sc.sb("vbuf", [P, 2, KT, NH, VC], F16)
        p32 = sc.sb("p32", [P, 3, HG * SQ])
        probs = sc.sb("probs", [P, 2, 2, KT, PW], F16)
        onehot = sc.sb("onehot", [P, HG], F16)
        nmax = sc.sb("nmax", [P, HG])
        nmax_parts = sc.sb("nmax_parts", [P, P], F16)
        pv_sb = sc.sb("pv_sb", [P, 2, HG, OC])
        orecip = sc.sb("orecip", [P, 2, HG])
        o32 = sc.sb("o32", [P, E])
        oparts = sc.sb("oparts", [P, 2, E], F16)
        next_w32 = [ctxT[:, i].rearrange("p a k s -> p (a k s)")[:, :2 * ET * E].bitcast(F32).rearrange("p (k n) -> p k n", n=E)
                    for i in range(len(next_weights))]
        next_loaded, next_hi_made = sc.sem("next_loaded"), sc.sem("next_hi_made")
        if layer == 0:
            osum = sc.sb("osum", [P, HG, DK])
            c32 = sc.sb("c32", [P, 3, E])
            cparts = sc.sb("cparts", [P, 2, 2, E], F16)
            stats = sc.sb("stats", [P, 3, 6])
            mv = sc.sb("mv", [P, KT, 2])
            var = sc.sb("var", [P, KT])
            half_power = sc.sb("half_power", [P, KT])
            rstd = sc.sb("rstd", [P, 2, KT])
            rdiag = sc.sb("rdiag", [P, KT, P])
            rrow = sc.sb("rrow", [P, 2, SK])
            kscaled = sc.sb("kscaled", [P, 2, SK])
        if queries:
            qT = kstack[0][:, 1].rearrange("p h s -> p (h s)")[:, :2 * ET * ROWS].rearrange("p (a m r) -> p a m r", a=2, m=ET)
            q_acc_ready, q_made, q_hi_made, q_lo_made, q_stored = (sc.sem(n) for n in (
                "q_acc_ready", "q_made", "q_hi_made", "q_lo_made", "q_stored"))
        p_proj = sc.ps("p_proj", [P, 2, 512])
        p_max = sc.ps("p_max", [P, 2, 512])
        p_sc = sc.ps("p_sc", [P, 2, 512])
        p_pv = sc.ps("p_pv", [P, 512])
        misc32 = sc.ps("misc", [P, 512])
        misc16 = misc32[:].bitcast(F16)

        padded, onehot_made, onehot_seeded, onehot_placed = (sc.sem(n) for n in (
            "padded", "onehot_made", "onehot_seeded", "onehot_placed"))
        bias_col = sc.sb("score_bias", [P, 1])
        (proj_ready, proj_freed, k_hi_made, k_lo_made, v_hi_made, max_ready, max_made, nm_hi_made, nm_made,
         misc_ready, misc_freed, sc_ready, exp_made, p_hi_made, pv_ready, pv_copied, recip_made,
         o_summed, o_normed, o_made, o_hi_made, o_lo_made) = (sc.sem(n) for n in (
             "proj_ready", "proj_freed", "k_hi_made", "k_lo_made", "v_hi_made", "max_ready", "max_made",
             "nm_hi_made", "nm_made", "misc_ready", "misc_freed", "sc_ready", "exp_made", "p_hi_made",
             "pv_ready", "pv_copied", "recip_made", "o_summed", "o_normed", "o_made",
             "o_hi_made", "o_lo_made"))
        p_lo_made = [sc.sem(f"p_lo_made{i}") for i in range(2)]
        stacked = [sc.sem(f"stacked{i}") for i in range(2)]
        q_loaded = [sc.sem(f"q_loaded{i}") for i in range(2)]
        ctxT_moved = [sc.sem(f"ctxT_moved{i}") for i in range(2)]
        if layer == 0:
            c_loaded = [sc.sem(f"c_loaded{i}") for i in range(3)]
            (c_hi_made, c_lo_made, stats_made, mv_made, var_made, rstd_made, rdiag_made) = (sc.sem(n) for n in (
                "c_hi_made", "c_lo_made", "stats_made", "mv_made", "var_made", "rstd_made", "rdiag_made"))
        blk = sc.block()

        def next_tiles(s, j):
            n = ET * len(next_weights)
            first = (NSLOT - n) // 2 + 1
            return [divmod(j - first, ET)] if isinstance(s, int) and s == U and first <= j < first + n else []

        def load_next_weights(sp):
            sp.wait_ge(proj_ready, NPROJ * U)
            for i, (src, _hi, _lo) in enumerate(next_weights):
                sp.dma_start(next_w32[i], src).then_inc(next_loaded, 16)

        def lo_count(u, g, t):
            return (u * NG + g) * (KT // 2) + (t // 2 + 1)

        def prob_lo(eng, u, g, t):
            r = KROWS[t]
            eng.wait_ge(p_hi_made, (u * NG + g) * KT + (t + 1))
            eng.tensor_tensor(probs[:r, g % 2, 1, t, :HG * SQ], p32[:r, t % 3, :], probs[:r, g % 2, 0, t, :HG * SQ],
                              ALU.subtract).then_inc(p_lo_made[t % 2], 1)

        def steps(eng, step):
            last_loop = U - 2 if layer == 0 else U
            for s in range(2):
                step(s, s % 2, sl.kind(s))
            with eng.Fori(1, last_loop // 2) as i:
                for par in range(2):
                    step(2 * i + par, par, sl.kind(2))
            for s in range(last_loop, U + 2):
                step(s, s % 2, sl.kind(s))

        @blk.sync
        def _(sp):
            def load_ctx_tile(b, t):
                if not (isinstance(b, int) and b * KT + t < 3):
                    sp.wait_ge(c_hi_made, b * KT + (t - 2))
                    sp.wait_ge(c_lo_made, b * KT + (t - 2))
                    sp.wait_ge(stats_made, b * KT + (t - 2))
                r = KROWS[t]
                sp.dma_start(c32[:r, t % 3, :], ctx_d[bass.ds(b, 1), P * t:P * t + r, :].rearrange("o p e -> (o p) e")
                             ).then_inc(c_loaded[t % 3], 16)

            def spill_ctx(b, par):
                sp.wait_ge(misc_freed, sl.misc_count(b - 1, ("ctx", KT - 1)))
                sp.dma_start(ctxT_d[bass.ds(b, 1)].rearrange("o p n -> (o p) n"), ctxT[:, par].rearrange("p a k s -> p (a k s)")
                             ).then_inc(ctxT_moved[par], 16)

            def load_ctxT(u, par, b):
                if not (isinstance(u, int) and u < 2):
                    sp.wait_ge(proj_ready, NPROJ * (u - 1))
                sp.dma_start(ctxT[:, par].rearrange("p a k s -> p (a k s)"), ctxT_d[bass.ds(b, 1)].rearrange("o p n -> (o p) n")
                             ).then_inc(ctxT_moved[par], 16)

            def load_q(u, par, b):
                if not (isinstance(u, int) and u < 2):
                    sp.wait_ge(sc_ready, NSLOT * (u - 1))
                h0 = 0 if layer == 0 else NH * par
                for i in range(NQ):
                    n = 96 if layer == 0 else (128, 64)[i]
                    sp.dma_start(qstack[i][:n, par], q_d[128 * i:128 * i + n, h0:h0 + NH, bass.ds(b * SQ, SQ)]).then_inc(q_loaded[par], 16)

            def stack_k(u, par, i):
                if layer == 0:
                    sp.wait_ge(k_lo_made, 4 * u + (2 * i + 2))
                else:
                    sp.wait_ge(proj_freed, NPROJ * u + (4 * i + 4))
                tiles = slice(2 * i, 2 * i + 2)
                for j in range(HPT):
                    heads = slice(2 * HPT * i + j, 2 * HPT * (i + 1), HPT)
                    part = lambda a: knat[DK * j:DK * j + DK, tiles, a, :]
                    if layer == 0:
                        for row, a in enumerate((0, 1, 0)):
                            sp.dma_start(kstack[0][DK * row:DK * row + DK, par, heads, :], part(a)).then_inc(stacked[i], 16)
                    else:
                        sp.dma_start(kstack[0][:DK, par, heads, :], part(0)).then_inc(stacked[i], 16)
                        sp.dma_start(kstack[0][DK:, par, heads, :], part(1)).then_inc(stacked[i], 16)
                        sp.dma_start(kstack[1][:DK, par, heads, :], part(0)).then_inc(stacked[i], 16)

            def place_onehot():
                sp.wait_ge(onehot_seeded, HG)
                rows = kstack[-1][MR:MR + 2 * HG]
                for par in range(2):
                    for g in range(NG):
                        if par or g:
                            sp.dma_start(rows[:, par, HG * g:HG * g + HG, :], rows[:, 0, 0:HG, :]).then_inc(onehot_placed, 16)

            if layer == 0:
                def step(s, par, kind):
                    prep, proj, _scores, _outs = kind
                    if prep and not (isinstance(s, int) and s == 0):
                        for t in range(3):
                            load_ctx_tile(s + 1, t)
                    if proj:
                        load_q(s, par, s)
                    for i in range(2):
                        if prep:
                            load_ctx_tile(s + 1, 3 + i)
                        if proj:
                            stack_k(s, par, i)
                    if prep:
                        load_ctx_tile(s + 1, 5)
                    if prep:
                        spill_ctx(s + 1, 1 - par)

                for t in range(KT):
                    load_ctx_tile(0, t)
                count = 0
                for m in range(ET):
                    if m == 2:
                        for t in range(3):
                            load_ctx_tile(1, t)
                    sp.wait_ge(q_lo_made, 2 * m + 2)
                    count += store_queries(sp, q_d, qT, m, q_stored)
                spill_ctx(0, 0)
                sp.wait_ge(q_stored, 16 * count)
                place_onehot()
                steps(sp, step)
                for i in range(2):
                    sp.wait_ge(ctxT_moved[i], 16 * (B // 2))
                load_next_weights(sp)
            else:
                def unit(u, par, b, ahead=True):
                    load_q(u, par, b)
                    for i in range(2):
                        stack_k(u, par, i)
                    if ahead:
                        load_ctxT(u + 2, par, b + 1)

                load_ctxT(0, 0, 0)
                load_ctxT(1, 1, 0)
                place_onehot()
                for u in range(2):
                    unit(u, u, 0)
                with sp.Fori(1, B - 1) as b:
                    for par in range(2):
                        unit(2 * b + par, par, b)
                for u in range(U - 2, U):
                    unit(u, u % 2, B - 1, ahead=False)
                load_next_weights(sp)

        @blk.tensor
        def _(pe):
            def misc_wait(s, use, first=False):
                if not first:
                    pe.wait_ge(misc_freed, sl.misc_count(s, use) - 1)

            def ctx_transposes(s, par, t):
                b, r = s + 1, KROWS[t]
                pe.wait_ge(c_hi_made, b * KT + (t + 1))
                pe.wait_ge(c_lo_made, b * KT + (t + 1))
                misc_wait(s, ("ctx", t), first=(isinstance(s, int) and s < 0 and t == 0))
                for a in range(2):
                    for k in range(ET):
                        o = (a * ET + k) * P
                        last = pe.transpose(misc16[:, o:o + r], cparts[:r, t % 2, a, k * P:(k + 1) * P], ident16[:r, :r])
                last.then_inc(misc_ready, 1)

            def rstd_rows(s, n):
                pe.wait_ge(rdiag_made, (s + 2) * KT)
                misc_wait(s, ("bc", n))
                for t in range(3 * n, 3 * n + 3):
                    r = KROWS[t]
                    o = P * (t - 3 * n)
                    last = pe.matmul(misc32[:, o:o + r], ones32[:r, :], rdiag[:r, t, :r], start=True, stop=True)
                last.then_inc(misc_ready, 1)

            def project(u, par, a):
                n_use = NPROJ * u + a
                if not (isinstance(u, int) and n_use < 2):
                    pe.wait_ge(proj_freed, NPROJ * u + (a - 1))
                if a == 0:
                    if layer == 1:
                        pe.wait_ge(ctxT_moved[par], 16 * (u // 2 + 1) if isinstance(u, int) else 8 * (u - par) + 16)
                    else:
                        pe.wait_ge(misc_freed, sl.misc_count(u - 1, ("ctx", KT - 1)))
                c0 = 0 if layer == 0 else E * par
                bank = p_proj[:, a % 2, :]
                j = 0
                for k in range(ET):
                    for wa, ca in PARTS:
                        flags = dict(start=(j == 0), stop=(j == 3 * ET - 1))
                        if a < 8:
                            m, n = divmod(a, 2)
                            last = pe.matmul(bank[:, :HALF], w_k[:, wa, k, c0 + m * P:c0 + (m + 1) * P],
                                             ctxT[:, par, ca, k, n * HALF:(n + 1) * HALF], **flags)
                        else:
                            t = a - 8
                            r = KROWS[t]
                            last = pe.matmul(bank[:r, :], ctxT[:, par, ca, k, P * t:P * t + r],
                                             w_v[:, wa, k, c0:c0 + E], **flags)
                        j += 1
                last.then_inc(proj_ready, 1)

            def max_scores(u, par, g, hh):
                n_use = (u * NG + g) * HG + hh
                h = HG * g + hh
                if hh == 0 and g == 0:
                    pe.wait_ge(q_loaded[par], 16 * NQ * (u // 2 + 1) if isinstance(u, int) else 8 * NQ * (u - par) + 16 * NQ)
                if h % (2 * HPT) == 0:
                    pe.wait_ge(stacked[h // (2 * HPT)], 16 * NSTACK * (u + 1))
                if not (isinstance(u, int) and n_use < 1):
                    pe.wait_ge(max_made, n_use)
                kr = MR if layer == 0 else P
                for n in range(2):
                    last = pe.matmul(p_max[:SQ, n, :HALF], qstack[0][:kr, par, h, :],
                                     kstack[0][:kr, par, h, n * HALF:(n + 1) * HALF], start=True, stop=True)
                last.then_inc(max_ready, 1)

            def max_transposes(s, G1, g):
                pe.wait_ge(nm_made, G1)
                misc_wait(s, ("max", g), first=(layer == 1 and isinstance(s, int) and s == 0))
                pe.transpose(misc16[:, :SQ], nmax_parts[:SQ, :], ident16[:SQ, :SQ]).then_inc(misc_ready, 1)

            def scores(s, u, par, g, t):
                n_use = (u * NG + g) * KT + t
                r = KROWS[t]
                if g == 0 and t == 0 and isinstance(u, int) and u == 0:
                    pe.wait_ge(onehot_placed, 16 * (2 * NG - 1))
                if t == 0:
                    pe.wait_ge(misc_freed, sl.misc_count(s, ("max", g - 1)) if g else sl.misc_count(s - 1, ("max", NG - 1)))
                if not (isinstance(u, int) and n_use < 2):
                    pe.wait_ge(exp_made, n_use - 1)
                for hh in range(HG):
                    h = HG * g + hh
                    out = p_sc[:r, t % 2, hh * SQ:(hh + 1) * SQ]
                    if layer == 0:
                        last = pe.matmul(out, kstack[0][:MR + 2 * HG, par, h, P * t:P * t + r],
                                         qstack[0][:MR + 2 * HG, par, h, :], start=True, stop=True)
                    else:
                        pe.matmul(out, kstack[0][:, par, h, P * t:P * t + r], qstack[0][:, par, h, :], start=True, stop=False)
                        last = pe.matmul(out, kstack[1][:MR + 2 * HG, par, h, P * t:P * t + r],
                                         qstack[1][:MR + 2 * HG, par, h, :], start=False, stop=True)
                last.then_inc(sc_ready, 1)

            def times_v(u, par, g, hh):
                G = u * NG + g
                if hh == 0:
                    for i in range(2):
                        pe.wait_ge(p_lo_made[i], (G + 1) * (KT // 2))
                    if g == 0:
                        pe.wait_ge(proj_freed, NPROJ * (u + 1))
                    if not (isinstance(u, int) and G == 0):
                        pe.wait_ge(pv_copied, G)
                h = HG * g + hh
                o = hh * OC
                for t in range(KT):
                    r = KROWS[t]
                    v = vbuf[:r, par, t, h, :]
                    ph, pl = (probs[:r, g % 2, a, t, hh * SQ:hh * SQ + P] for a in range(2))
                    first, end = t == 0, t == KT - 1
                    if layer == 0:
                        pe.matmul(p_pv[:, o:o + OC], ph, v, start=first, stop=False)
                        last = pe.matmul(p_pv[:, o:o + OC], pl, v, start=False, stop=end)
                    else:
                        pe.matmul(p_pv[:, o:o + OC], ph, v[:, :OC], start=first, stop=False)
                        pe.matmul(p_pv[:, o:o + DK], ph, v[:, OC:], start=False, stop=False)
                        last = pe.matmul(p_pv[:, o:o + OC], pl, v[:, :OC], start=False, stop=end)
                if hh == HG - 1:
                    last.then_inc(pv_ready, 1)

            def out_transposes(s):
                pe.wait_ge(o_lo_made, s - 1)
                misc_wait(s, ("out", 0))
                for a in range(2):
                    for k in range(ET):
                        o = (a * ET + k) * P
                        last = pe.transpose(misc16[:, o:o + SQ], oparts[:SQ, a, k * P:(k + 1) * P], ident16[:SQ, :SQ])
                last.then_inc(misc_ready, 1)

            def step(s, par, kind):
                prep, proj, has_scores, outs = kind
                for j in range(sl.n):
                    g, t = divmod(j, KT)
                    if g < NG - 1 and has_scores and t < HG:
                        max_scores(s - 1, 1 - par, g + 1, t)
                    if g == NG - 1 and proj and t < HG:
                        max_scores(s, par, 0, t)
                    if has_scores:
                        scores(s, s - 1, 1 - par, g, t)
                    if prep and j in sl.ctx:
                        ctx_transposes(s, par, sl.ctx[j])
                    if prep and j in sl.bc:
                        rstd_rows(s, sl.bc[j])
                    if outs and j == sl.out_t:
                        out_transposes(s)
                    if g < NG - 1 and has_scores and t == MAX_T:
                        max_transposes(s, (s - 1) * NG + (g + 2), g)
                    if g == NG - 1 and proj and t == MAX_T:
                        max_transposes(s, s * NG + 1, g)
                    if 0 <= t - PV_T < HG:
                        if g == 0 and outs:
                            times_v(s - 2, par, NG - 1, t - PV_T)
                        if g > 0 and has_scores:
                            times_v(s - 1, 1 - par, g - 1, t - PV_T)
                    if proj:
                        for a in sl.proj[j]:
                            project(s, par, a)

            def project_queries(u):
                xT, w, _bias, _scale = queries
                m, n = divmod(u, 2)
                if u >= 2:
                    pe.wait_ge(q_made, u - 1)
                for k in range(ET):
                    for i, (wa, xa) in enumerate(PARTS):
                        last = pe.matmul(p_sc[:, n, :QHALF], w[:, wa, k, m * P:(m + 1) * P],
                                         xT[:, xa, k, n * QHALF:(n + 1) * QHALF], start=(k + i == 0), stop=(k == ET - 1 and i == 2))
                last.then_inc(q_acc_ready, 1)

            if layer == 0:
                for u in range(2 * ET):
                    project_queries(u)
                    if u < KT:
                        ctx_transposes(-1, 1, u)
                for n in range(2):
                    rstd_rows(-1, n)
                pe.wait_ge(q_made, 2 * ET)
            steps(pe, step)

        @blk.scalar
        def _(act):
            def ctx_hi(b, t):
                r = KROWS[t]
                act.wait_ge(c_loaded[t % 3], 32 * b + 16 * (t // 3 + 1))
                if not (isinstance(b, int) and b == 0 and t < 2):
                    act.wait_ge(misc_ready, sl.misc_count(b - 1, ("ctx", t - 2)) if t >= 2 else sl.misc_count(b - 2, ("ctx", KT - 2 + t)))
                act.copy(cparts[:r, t % 2, 0, :], c32[:r, t % 3, :]).then_inc(c_hi_made, 1)

            def rstd_row(s, par, n):
                act.wait_ge(misc_ready, sl.misc_count(s, ("bc", n)))
                c = slice(0, 3 * P) if n == 0 else slice(3 * P, SK)
                act.copy(rrow[:, 1 - par, c], misc32[:, :c.stop - c.start]).then_inc(misc_freed, 1)

            def exp(u, g, t):
                n_use = (u * NG + g) * KT + t
                r = KROWS[t]
                act.wait_ge(sc_ready, n_use + 1)
                if not (isinstance(u, int) and n_use < 3):
                    act.wait_ge(p_lo_made[1 - t % 2], lo_count(u, g, t - 3))
                act.activation(p32[:r, t % 3, :], p_sc[:r, t % 2, :HG * SQ], ACT.Exp,
                               bias=bias_col[:r, 0:1] if score_bias else 0.0).then_inc(exp_made, 1)

            def prob_hi(u, g, t):
                n_use = (u * NG + g) * KT + t
                r = KROWS[t]
                act.wait_ge(exp_made, n_use + 1)
                G = u * NG + g
                if t == 0 and not (isinstance(u, int) and G < 2):
                    act.wait_ge(pv_ready, G - 1)
                act.copy(probs[:r, g % 2, 0, t, :HG * SQ], p32[:r, t % 3, :]).then_inc(p_hi_made, 1)

            def evacuate(u, par, a):
                if a < 8:
                    m, n = divmod(a, 2)
                    if layer == 0:
                        if n == 0:
                            return
                        act.wait_ge(proj_freed, NPROJ * u + (a + 1))
                        cols = slice(0, SK)
                        src = kscaled[:, m % 2, :]
                    else:
                        act.wait_ge(proj_ready, NPROJ * u + (a + 1))
                        cols = slice(n * HALF, (n + 1) * HALF)
                        src = p_proj[:, a % 2, :HALF]
                    if n == 0 or layer == 0:
                        if m % 2 == 0 and not (isinstance(u, int) and u == 0):
                            act.wait_ge(stacked[m // 2], 16 * NSTACK * u)
                    if layer == 0:
                        act.activation(knat[:, m, 0, cols], src, ACT.Identity, bias=kb_col[:, m:m + 1]).then_inc(k_hi_made, 1)
                    else:
                        act.activation(knat[:, m, 0, cols], src, ACT.Identity, scale=1.0 / WS).then_inc(k_hi_made, 1)
                else:
                    t = a - 8
                    r = KROWS[t]
                    act.wait_ge(proj_ready, NPROJ * u + (a + 1))
                    if t == 0 and not (isinstance(u, int) and u < 2):
                        act.wait_ge(pv_ready, (u - 1) * NG)
                    scale = rstd[:r, par, t:t + 1] if layer == 0 else 1.0 / WS
                    act.activation(vbuf[:r, par, t, :, 0:DK], p_proj[:r, a % 2, :].rearrange("p (h d) -> p h d", d=DK),
                                   ACT.Identity, scale=scale).then_inc(v_hi_made, 1)

            def out_hi(s):
                act.wait_ge(o_made, (s - 1) * NG)
                if not (isinstance(s, int) and s == 2):
                    act.wait_ge(misc_ready, sl.misc_count(s - 1, ("out", 0)))
                act.copy(oparts[:SQ, 0, :], o32[:SQ, :]).then_inc(o_hi_made, 1)

            def step(s, par, kind):
                prep, proj, has_scores, outs = kind
                for j in range(sl.n):
                    g, t = divmod(j, KT)
                    if has_scores:
                        exp(s - 1, g, t)
                        if j > 0:
                            prob_hi(s - 1, *divmod(j - 1, KT))
                    if prep and j + 2 in sl.ctx:
                        ctx_hi(s + 1, sl.ctx[j + 2])
                    if prep and j in sl.bc:
                        rstd_row(s, par, sl.bc[j])
                    if outs and j == sl.out_t - 2:
                        out_hi(s)
                    for i, k in next_tiles(s, j):
                        act.wait_ge(next_loaded, 16 * len(next_weights))
                        act.activation(next_weights[i][1][:, k], next_w32[i][:, k], ACT.Identity, scale=WS).then_inc(next_hi_made, 1)
                    if proj:
                        for a in sl.evac[j]:
                            evacuate(s, par, a)
                if has_scores:
                    prob_hi(s - 1, NG - 1, KT - 1)

            act.wait_ge(padded, 1)
            if layer == 0:
                for u in range(2 * ET):
                    if u < KT:
                        ctx_hi(0, u)
                    act.wait_ge(q_acc_ready, u + 1)
                    if u >= 3:
                        act.wait_ge(q_lo_made, u - 2)
                    act.activation(p32[:, u % 3, :], p_sc[:, u % 2, :QHALF], ACT.Identity, bias=queries[2][:, u // 2:u // 2 + 1],
                                   scale=queries[3]).then_inc(q_made, 1)
                for n in range(2):
                    rstd_row(-1, 1, n)
                act.wait_ge(q_lo_made, 2 * ET)
            steps(act, step)

        @blk.vector
        def _(dve):
            def ctx_stats(b, t):
                r = KROWS[t]
                if t == 0 and not (isinstance(b, int) and b == 0):
                    dve.wait_ge(var_made, b)
                dve.wait_ge(c_loaded[t % 3], 32 * b + 16 * (t // 3 + 1))
                dve.bn_stats(stats[:r, t % 3, :], c32[:r, t % 3, :]).then_inc(stats_made, 1)
                dve.drain()
                dve.bn_aggr(mv[:r, t, :], stats[:r, t % 3, :]).then_inc(mv_made, 1)

            def ctx_var(b):
                dve.wait_ge(mv_made, (b + 1) * KT)
                if not (isinstance(b, int) and b == 0):
                    dve.wait_ge(rstd_made, b)
                dve.tensor_scalar(var[:], mv[:, :, 1], eps, WS * WS, ALU.add, ALU.mult).then_inc(var_made, 1)

            def rstd_diag(b, par):
                dve.wait_ge(rstd_made, b + 1)
                if not (isinstance(b, int) and b == 0):
                    dve.wait_ge(misc_ready, sl.misc_count(b - 2, ("bc", 1)))
                for t in range(KT):
                    r = KROWS[t]
                    dve.tensor_scalar(rdiag[:r, t, :], ident[:r, :], rstd[:r, par, t:t + 1], None, ALU.mult).then_inc(rdiag_made, 1)

            def ctx_copy(s, par, t):
                r = KROWS[t]
                dve.wait_ge(misc_ready, sl.misc_count(s, ("ctx", t)))
                if t == 0 and not (isinstance(s, int) and s < 1):
                    dve.wait_ge(proj_ready, NPROJ * s)
                    dve.wait_ge(ctxT_moved[1 - par], 16 * ((s + 1) // 2) if isinstance(s, int) else 8 * (s - par) + 16 * par)
                dve.tensor_copy(ctxT[:, 1 - par, :, :, P * t:P * t + r],
                                misc16.rearrange("p (a k s) -> p a k s", a=2, k=ET)[:, :, :, :r]).then_inc(misc_freed, 1)

            def take_max(u, g, hh):
                n_use = (u * NG + g) * HG + hh
                dve.wait_ge(max_ready, n_use + 1)
                if hh == 0 and not (isinstance(u, int) and n_use == 0):
                    dve.wait_ge(nm_made, u * NG + g)
                dve.tensor_reduce(nmax[:SQ, hh:hh + 1], p_max[:SQ, :, :HALF], AX.XY, ALU.max, negate=True).then_inc(max_made, 1)

            def split_max(s, u, g, prev):
                G = u * NG + g
                dve.wait_ge(max_made, (G + 1) * HG)
                if prev is not None:
                    dve.wait_ge(misc_ready, prev)
                dve.tensor_scalar(nmax_parts[:SQ, MR:MR + HG], nmax[:SQ, :], -score_bias, None, ALU.add).then_inc(nm_hi_made, 1)
                dve.wait_ge(nm_hi_made, G + 1)
                dve.scalar_tensor_tensor(nmax_parts[:SQ, MR + HG:MR + 2 * HG], nmax[:SQ, :], -score_bias,
                                         nmax_parts[:SQ, MR:MR + HG], ALU.add, ALU.subtract).then_inc(nm_made, 1)

            def place_max(s, use, par, g):
                dve.wait_ge(misc_ready, sl.misc_count(s, use))
                src = misc16[MR:MR + 2 * HG, :SQ].rearrange("p (o q) -> p o q", o=1).to_broadcast([2 * HG, HG, SQ])
                dve.tensor_copy(qstack[-1][MR:MR + 2 * HG, par, HG * g:HG * g + HG, :], src).then_inc(misc_freed, 1)

            def k_lo(u, m):
                dve.wait_ge(k_hi_made, 4 * u + (m + 1))
                dve.scalar_tensor_tensor(knat[:, m, 1, :], kscaled[:, m % 2, :], kb_col[:, m:m + 1],
                                         knat[:, m, 0, :], ALU.add, ALU.subtract).then_inc(k_lo_made, 1)

            def evacuate(u, par, a):
                if a < 8:
                    m, n = divmod(a, 2)
                    cols = slice(n * HALF, (n + 1) * HALF)
                    if layer == 0:
                        dve.wait_ge(proj_ready, NPROJ * u + (a + 1))
                        if n == 0:
                            if a == 0:
                                dve.wait_ge(misc_freed, sl.misc_count(u - 1, ("bc", 1)))
                            if not (isinstance(u, int) and 4 * u + m < 2):
                                dve.wait_ge(k_hi_made, 4 * u + (m - 1))
                                dve.wait_ge(k_lo_made, 4 * u + (m - 1))
                        dve.tensor_tensor(kscaled[:, m % 2, cols], p_proj[:, a % 2, :HALF], rrow[:, par, cols],
                                          ALU.mult).then_inc(proj_freed, 1)
                    else:
                        dve.wait_ge(k_hi_made, 8 * u + (a + 1))
                        ins = dve.scalar_tensor_tensor(knat[:, m, 1, cols], p_proj[:, a % 2, :HALF], 1.0 / WS,
                                                       knat[:, m, 0, cols], ALU.mult, ALU.subtract)
                        ins.then_inc(proj_freed, 1)
                else:
                    t = a - 8
                    r = KROWS[t]
                    dve.wait_ge(v_hi_made, KT * u + (t + 1))
                    scale = rstd[:r, par, t:t + 1] if layer == 0 else 1.0 / WS
                    dve.scalar_tensor_tensor(vbuf[:r, par, t, :, DK + 1:], p_proj[:r, a % 2, :].rearrange("p (h d) -> p h d", d=DK),
                                             scale, vbuf[:r, par, t, :, 0:DK], ALU.mult, ALU.subtract).then_inc(proj_freed, 1)

            def copy_pv(u, g):
                G = u * NG + g
                dve.wait_ge(pv_ready, G + 1)
                if not (isinstance(u, int) and G < 2):
                    dve.wait_ge(o_normed if layer == 0 else o_made, G - 1)
                dve.tensor_copy(pv_sb[:SQ, g % 2, :, :], p_pv[:SQ, :HG * OC].rearrange("p (h c) -> p h c", c=OC)).then_inc(pv_copied, 1)
                dve.wait_ge(pv_copied, G + 1)
                dve.reciprocal(orecip[:SQ, g % 2, :], pv_sb[:SQ, g % 2, :, DK]).then_inc(recip_made, 1)

            def out_copy(s, par, b):
                dve.wait_ge(misc_ready, sl.misc_count(s, ("out", 0)))
                src = misc16.rearrange("p (a k s) -> p a k s", a=2, k=ET)[:, :, :, :SQ]
                out = outT[0 if layer == 0 else par]
                dve.tensor_copy(out[:, :, :, bass.ds(b * SQ, SQ)], src).then_inc(misc_freed, 1)

            def step(s, par, kind, batch=None):
                prep, proj, has_scores, outs = kind
                for j in range(sl.n):
                    g, t = divmod(j, KT)
                    if g < NG - 1:
                        nxt = (s - 1, g + 1) if has_scores else None
                    else:
                        nxt = (s, 0) if proj else None
                    if nxt and t < HG:
                        take_max(*nxt, t)
                        if t == HG - 1:
                            if g > 0:
                                prev = sl.misc_count(s, ("max", g - 1)) if has_scores else None
                            else:
                                prev = sl.misc_count(s - 1, ("max", NG - 1))
                            split_max(s, *nxt, prev)
                    if prep and j in sl.ctx:
                        ctx_copy(s, par, sl.ctx[j])
                    if prep and j + 2 in sl.ctx:
                        ctx_stats(s + 1, sl.ctx[j + 2])
                    if prep and j == sl.var_t:
                        ctx_var(s + 1)
                    if prep and j == sl.diag_t:
                        rstd_diag(s + 1, 1 - par)
                    if outs and j == sl.out_t:
                        out_copy(s, par, s - 2 if layer == 0 else batch)
                    if has_scores and j > 0 and (t - 1) % 2:
                        prob_lo(dve, s - 1, *divmod(j - 1, KT))
                    if t == MAX_T:
                        if g < NG - 1 and has_scores:
                            place_max(s, ("max", g), 1 - par, g + 1)
                        if g == NG - 1 and proj:
                            place_max(s, ("max", g), par, 0)
                    if t == PV_T + HG - 1:
                        if g == 0 and outs:
                            copy_pv(s - 2, NG - 1)
                        if g > 0 and has_scores:
                            copy_pv(s - 1, g - 1)
                    for i, k in next_tiles(s, j):
                        dve.wait_ge(next_hi_made, ET * i + (k + 1))
                        dve.scalar_tensor_tensor(next_weights[i][2][:, k], next_w32[i][:, k], WS, next_weights[i][1][:, k],
                                                 ALU.mult, ALU.subtract)
                    if proj:
                        if layer == 0 and j in sl.k_lo:
                            k_lo(s, sl.k_lo[j])
                        for a in sl.evac[j]:
                            evacuate(s, par, a)
                if has_scores:
                    prob_lo(dve, s - 1, NG - 1, KT - 1)

            def split_queries(u):
                m, n = divmod(u, 2)
                cols = slice(n * QHALF, (n + 1) * QHALF)
                dve.wait_ge(q_made, u + 1)
                dve.tensor_copy(qT[:, 0, m, cols], p32[:, u % 3, :]).then_inc(q_hi_made, 1)
                dve.wait_ge(q_hi_made, u + 1)
                dve.tensor_tensor(qT[:, 1, m, cols], p32[:, u % 3, :], qT[:, 0, m, cols], ALU.subtract).then_inc(q_lo_made, 1)

            dve.tensor_tensor(onehot[MR:MR + 2 * HG, :], ident[MR:MR + 2 * HG, MR:MR + HG],
                              ident[MR:MR + 2 * HG, MR + HG:MR + 2 * HG], ALU.add).then_inc(onehot_made, 1)
            dve.memset(probs[:, :, :, :, HG * SQ:], 0.0)
            dve.memset(nmax_parts[:], 0.0)
            if layer == 0:
                dve.memset(mv[:], 1.0)
                dve.memset(half_power[:], -0.5)
            dve.memset(vbuf[:, :, :, :, DK:DK + 1], 1.0)
            dve.memset(bias_col[:], score_bias).then_inc(padded, 1)
            dve.wait_ge(onehot_made, 1)
            for hh in range(HG):
                dve.tensor_copy(kstack[-1][MR:MR + 2 * HG, 0, hh, :],
                                onehot[MR:MR + 2 * HG, hh:hh + 1].to_broadcast([2 * HG, SK])).then_inc(onehot_seeded, 1)
            dve.wait_ge(padded, 1)
            if layer == 0:
                for t in range(KT):
                    ctx_stats(0, t)
                    if t >= 1:
                        ctx_copy(-1, 1, t - 1)
                        split_queries(t - 1)
                ctx_copy(-1, 1, KT - 1)
                ctx_var(0)
                rstd_diag(0, 0)
                for u in range(KT - 1, 2 * ET):
                    split_queries(u)
                steps(dve, step)
            else:
                for s in range(2):
                    step(s, s, sl.kind(s))
                with dve.Fori(1, U // 2) as i:
                    for par in range(2):
                        step(2 * i + par, par, sl.kind(2), i - 1)
                for s in range(U, U + 2):
                    step(s, s % 2, sl.kind(s), s // 2 - 1)

        @blk.gpsimd
        def _(pool):
            def ctx_lo(b, t):
                r = KROWS[t]
                pool.wait_ge(c_hi_made, b * KT + (t + 1))
                pool.tensor_tensor(cparts[:r, t % 2, 1, :], c32[:r, t % 3, :], cparts[:r, t % 2, 0, :], ALU.subtract).then_inc(c_lo_made, 1)

            def ctx_rstd(b, par):
                pool.wait_ge(var_made, b + 1)
                if not (isinstance(b, int) and b < 2):
                    pool.wait_ge(proj_freed, NPROJ * (b - 1))
                pool.tensor_tensor(rstd[:, par, :], var[:], half_power[:], ALU.pow).then_inc(rstd_made, 1)

            def normalise(u, g):
                G = u * NG + g
                cols = slice(g * HG * DK, (g + 1) * HG * DK)
                out = o32[:SQ, cols].rearrange("p (h d) -> p h d", d=DK)
                recip = orecip[:SQ, g % 2, :].rearrange("p (h o) -> p h o", o=1).to_broadcast([SQ, HG, DK])
                pool.wait_ge(recip_made, G + 1)
                if g == 0 and not (isinstance(u, int) and u == 0):
                    pool.wait_ge(o_lo_made, u)
                if layer == 0:
                    pool.tensor_tensor(osum[:SQ], pv_sb[:SQ, g % 2, :, :DK], pv_sb[:SQ, g % 2, :, DK + 1:], ALU.add).then_inc(o_summed, 1)
                    pool.wait_ge(o_summed, G + 1)
                    pool.tensor_tensor(osum[:SQ], osum[:SQ], recip, ALU.mult).then_inc(o_normed, 1)
                    pool.wait_ge(o_normed, G + 1)
                    pool.tensor_tensor(o32[:SQ, cols], osum[:SQ].rearrange("p h d -> p (h d)"), vb_row[:SQ, cols], ALU.add).then_inc(o_made, 1)
                    pool.wait_ge(o_made, G + 1)
                else:
                    pool.tensor_tensor(out, pv_sb[:SQ, g % 2, :, :DK], recip, ALU.mult).then_inc(o_made, 1)

            def out_lo(s):
                pool.wait_ge(o_hi_made, s - 1)
                pool.tensor_tensor(oparts[:SQ, 1, :], o32[:SQ, :], oparts[:SQ, 0, :], ALU.subtract).then_inc(o_lo_made, 1)

            def step(s, par, kind):
                prep, proj, has_scores, outs = kind
                for j in range(sl.n):
                    g, t = divmod(j, KT)
                    if has_scores and j > 0 and (t - 1) % 2 == 0:
                        prob_lo(pool, s - 1, *divmod(j - 1, KT))
                    if prep and j + 2 in sl.ctx:
                        ctx_lo(s + 1, sl.ctx[j + 2])
                    if prep and j == sl.var_t:
                        ctx_rstd(s + 1, 1 - par)
                    if t == PV_T + HG - 1:
                        if g == 0 and outs:
                            normalise(s - 2, NG - 1)
                        if g > 0 and has_scores:
                            normalise(s - 1, g - 1)
                    if outs and j == sl.out_t - 1:
                        out_lo(s)

            if layer == 0:
                for t in range(KT):
                    ctx_lo(0, t)
                ctx_rstd(0, 0)
            steps(pool, step)


def bass_two_cross_attentions(nc, x, ctx, wq, bq, wk, bk, wv, bv, wo, bo, ln1_g, ln1_b, ln2_g, ln2_b, w1, b1, w2, b2,
                              wq1, wk1, wv1, wfc, gamma, beta, out):
    rows = lambda a: a.rearrange("b s e -> (b s) e")
    by_tile = lambda w: w.rearrange("(k p) n -> p k n", p=P)
    x_rows, out_rows = rows(x), rows(out)
    q0_d = nc.dram_tensor("q0_stack", [3 * 32, H, ROWS], F16, kind="Internal").ap()
    q1_d = nc.dram_tensor("q1_stack", [3 * 64, H, ROWS], F16, kind="Internal").ap()
    ctxT_d = nc.dram_tensor("ctxT_parts", [B, P, 2 * ET * SK], F16, kind="Internal").ap()
    x2_d = nc.dram_tensor("layer0_out", [ROWS, E], F32, kind="Internal").ap()

    def columns(w):
        v = by_tile(w)
        return [v[:, :, c:c + E] for c in range(0, w.shape[1], E)]

    def part_jobs(pieces, parts):
        return [(piece, parts[:, 0, :, c * E:(c + 1) * E], parts[:, 1, :, c * E:(c + 1) * E]) for c, piece in enumerate(pieces)]

    def tile_jobs(w, parts, step):
        v = by_tile(w)
        return [(v[:, k:k + step, :], parts[:, 0, k:k + step, :], parts[:, 1, k:k + step, :]) for k in range(0, v.shape[1], step)]

    with Scope(nc, "kernel") as top:
        ident = top.sb("ident", [P, P])
        ident16 = top.sb("ident16", [P, P], F16)
        ones_mean = top.sb("ones_mean", [P, P])
        ones32 = top.sb("ones32", [P, P])
        make_constants(nc, ident, ident16, ones_mean, ones32)

        x_parts = top.sb("x_parts", [P, 2, ET, ROWS], F16)
        w_qo = top.sb("w_qo", [P, 2, ET, E], F16)
        with Scope(nc, "l0") as l0:
            w_k = l0.sb("w_k", [P, 2, ET, E], F16)
            w_v = l0.sb("w_v", [P, 2, ET, E], F16)
            bqs_col = l0.sb("bqs_col", [P, ET])
            kb_col = l0.sb("kb_col", [P, ET])
            vb_row = l0.sb("vb_row", [P, E])
            with Scope(nc, "q0") as q0:
                g_row, b_row, bv_row = (q0.sb(n, [P, E]) for n in ("g_row", "b_row", "bv_row"))
                g_col, b_col, bk_col, bq_col = (q0.sb(n, [P, ET]) for n in ("g_col", "b_col", "bk_col", "bq_col"))
                scale0 = 32.0 ** -0.5
                rows_stage(nc, "rows_q0", ident16, x_rows, norm=(1e-5, g_row, b_row), xT=x_parts,
                           vectors=[(g_row, ln1_g), (b_row, ln1_b)], late_vectors=[(bv_row, bv), (g_col, ln1_g), (b_col, ln1_b),
                                    (bk_col, bk), (bq_col, bq)],
                           split=part_jobs(columns(wq), w_qo),
                           fold=((by_tile(wk), by_tile(wv)), g_col, b_col, bk_col, bv_row, bq_col, bqs_col, scale0,
                                 ones_mean, (w_k, w_v), kb_col, vb_row))
            attention(nc, 0, ctx, ctxT_d, q0_d, w_k, w_v, kb_col, vb_row, ident, ident16, ones32, 1e-5, 0.0, [x_parts],
                      next_weights=part_jobs(columns(wo), w_qo), queries=(x_parts, w_qo, bqs_col, scale0 / WS))
        with Scope(nc, "kv1") as kv1:
            w_k = kv1.sb("w_k", [P, 2, ET, 2 * E], F16)
            w_v = kv1.sb("w_v", [P, 2, ET, 2 * E], F16)
            with Scope(nc, "mlp") as m:
                w1p = m.sb("w1", [P, 2, ET, FF], F16)
                x1 = m.sb("x1", [P, RT, E])
                b2_row = m.sb("b2_row", [P, E])
                b1_col = m.sb("b1_col", [P, FT])
                with Scope(nc, "proj0") as pr:
                    g_row, b_row, bo_row = (pr.sb(n, [P, E]) for n in ("g_row", "b_row", "bo_row"))
                    rows_stage(nc, "rows_wo", ident16, x_rows, w=w_qo, lhs=[x_parts], bias=bo_row, norm=(1e-5, g_row, b_row),
                               keep=x1, xT=x_parts,
                               vectors=[(bo_row, bo), (g_row, ln2_g), (b_row, ln2_b)], late_vectors=[(b2_row, b2), (b1_col, b1)],
                               split=[(src[:, k:k + 2], hi[:, k:k + 2], lo[:, k:k + 2]) for src, hi, lo in part_jobs(columns(w1), w1p)
                                      for k in range(0, ET, 2)])
                hT = m.sb("hT", [P, 2, FT, ROWS], F16)
                w2p = m.sb("w2", [P, 2, FT, E], F16)
                columns_stage(nc, "cols_w1", x_parts, w1p, FT, ACT.Gelu, b1_col, 1.0 / WS, hT,
                              split=tile_jobs(w2, w2p, ET))
                w_q = w1p[:, :, :, 0:2 * E]
                rows_stage(nc, "rows_w2", ident16, None, w=w2p, lhs=[hT], res=x1, bias=b2_row, keep=x1, store=x2_d, xT=x_parts,
                           split=part_jobs(columns(wq1), w_q))
                columns_stage(nc, "cols_q1", x_parts, w_q, 2 * ET, ACT.Identity, None, 64.0 ** -0.5 / WS, hT[:, :, 0:2 * ET],
                              store=q1_d, split=part_jobs(columns(wk1), w_k) + part_jobs(columns(wv1), w_v))
            with Scope(nc, "attn_out1") as keep1:
                o1_parts = [x_parts, keep1.sb("o1_upper", [P, 2, ET, ROWS], F16)]
                w_fc = w_k[:].rearrange("p a k (c n) -> p a (k c) n", c=2)
                score_bias = -0.5 * 2.0 ** 2 / (0.5 * 4.0) ** 2
                attention(nc, 1, ctx, ctxT_d, q1_d, w_k, w_v, None, None, ident, ident16, ones32, None, score_bias, o1_parts,
                          next_weights=tile_jobs(wfc, w_fc, ET))
                g_row, b_row = keep1.sb("g_row", [P, E]), keep1.sb("b_row", [P, E])
                rows_stage(nc, "rows_fc", ident16, x2_d, w=w_fc, lhs=o1_parts, norm=(1e-6, g_row, b_row), store=out_rows,
                           vectors=[(g_row, gamma), (b_row, beta)])


_INS = ["x", "ctx_1024", "L0_xattn_wq", "L0_xattn_bq", "L0_xattn_wk", "L0_xattn_bk", "L0_xattn_wv", "L0_xattn_bv",
        "L0_xattn_wo", "L0_xattn_bo", "L0_xattn_ln1_g", "L0_xattn_ln1_b", "L0_xattn_ln2_g", "L0_xattn_ln2_b",
        "L0_xattn_w1", "L0_xattn_b1", "L0_xattn_w2", "L0_xattn_b2", "L1_xattn_Wq", "L1_xattn_Wk", "L1_xattn_Wv",
        "L1_xattn_Wfc", "L1_xattn_gamma", "L1_xattn_beta"]


def kernel(**inputs):
    import numpy as _np
    import concourse.bacc as _bacc
    from concourse import mybir as _mybir
    from concourse.bass_utils import run_bass_kernel_spmd as _run

    nc = _bacc.Bacc("TRN2", target_bir_lowering=False, num_devices=1)
    arrays, args = {}, []
    for name in _INS:
        a = _np.ascontiguousarray(inputs[name])
        arrays[f"in_{name}_dram"] = a
        args.append(nc.dram_tensor(f"in_{name}_dram", a.shape, _mybir.dt.from_np(a.dtype), kind="ExternalInput").ap())
    args.append(nc.dram_tensor("out_0_dram", (B, SQ, E), F32, kind="ExternalOutput").ap())
    bass_two_cross_attentions(nc, *args)
    r = _run(nc, [arrays], core_ids=[0])
    return r.results[0]["out_0_dram"]
```
